# Optimizing a Trainium2 kernel written in Bass

```python
import numpy as np
import jax
import jax.numpy as jnp

def _softmax(x, axis=-1):
    return jax.nn.softmax(x, axis=axis)

def _gelu(x):
    return jax.nn.gelu(x, approximate=True)

def _silu(x):
    return jax.nn.silu(x)

def _sigmoid(x):
    return jax.nn.sigmoid(x)

def _layernorm(x, axis=-1, eps=1e-05):
    m = jnp.mean(x, axis=axis, keepdims=True)
    v = jnp.var(x, axis=axis, keepdims=True)
    return (x - m) / jnp.sqrt(v + eps)

def _scatter_add(tgt, idx, src, axis=0):
    return tgt.at[idx].add(src)

def _segment_sum(src, seg, n):
    return jax.ops.segment_sum(src, seg, n)
kernel_name = 'mk_gnn_preln_d2_gnn_r8_e8ad5f'

def setup_inputs(seed: int=0):
    np.random.seed(seed)
    _w = jnp.asarray

    def _rec_inputs():
        import jax
        import jax.numpy as jnp
        _gk = jax.random.key(seed)
        x = -0.0003713 + 1 * jax.random.normal(jax.random.fold_in(_gk, 1), (12500, 128), jnp.float32)
        src = jax.random.randint(jax.random.fold_in(_gk, 2), (200000,), 0, 12500, jnp.int32)
        dst = jax.random.randint(jax.random.fold_in(_gk, 3), (200000,), 0, 12500, jnp.int32)
        _o = jnp.argsort(dst, stable=True)
        src = src[_o]
        dst = dst[_o]
        edge_attr_64 = 0.000135552 + 1.00015 * jax.random.normal(jax.random.fold_in(_gk, 11), (200000, 64), jnp.float32)
        edge_weight = jax.random.uniform(jax.random.fold_in(_gk, 13), (200000,), jnp.float32, 0.0, 999.998)
        node_vec = jax.random.uniform(jax.random.fold_in(_gk, 14), (12500,), jnp.float32, 0.0, 999.994)
        return (x, src, dst, edge_attr_64, edge_weight, node_vec)
    x, src, dst, edge_attr_64, edge_weight, node_vec = _rec_inputs()

    def _L0_gnn_setup():
        import jax, jax.numpy as jnp
        import numpy as np
        import math
        N = 12500
        E = 100000
        IN = 128
        OUT = 128
        MSG = 64
        TDIM = 32
        HEADS = 2
        CH = OUT // HEADS
        EDGE_DIM = MSG + TDIM
        key = jax.random.key(seed)
        ks = jax.random.split(key, 16)
        s = 1.0 / math.sqrt(IN)
        se = 1.0 / math.sqrt(EDGE_DIM)
        return {'x': jax.random.normal(ks[0], (N, IN), jnp.float32), 'last_update': jax.random.uniform(ks[1], (N,), jnp.float32, 0.0, 1000.0), 't': jax.random.uniform(ks[2], (E,), jnp.float32, 0.0, 1000.0), 'msg': jax.random.normal(ks[3], (E, MSG), jnp.float32), 'edge_index': jax.random.randint(ks[4], (2, E), 0, N, jnp.int32), 'time_w': jax.random.normal(ks[5], (TDIM,), jnp.float32), 'time_b': jax.random.normal(ks[6], (TDIM,), jnp.float32) * 0.1, 'Wq': jax.random.normal(ks[7], (IN, OUT), jnp.float32) * s, 'bq': jnp.zeros((OUT,), jnp.float32), 'Wk': jax.random.normal(ks[8], (IN, OUT), jnp.float32) * s, 'bk': jnp.zeros((OUT,), jnp.float32), 'Wv': jax.random.normal(ks[9], (IN, OUT), jnp.float32) * s, 'bv': jnp.zeros((OUT,), jnp.float32), 'We': jax.random.normal(ks[10], (EDGE_DIM, OUT), jnp.float32) * se, 'Wskip': jax.random.normal(ks[11], (IN, OUT), jnp.float32) * s, 'bskip': jnp.zeros((OUT,), jnp.float32)}
    _L0_gnn_all = _L0_gnn_setup()
    _L0_gnn_in = {k: v for k, v in _L0_gnn_all.items() if k in ('time_w', 'time_b', 'Wq', 'bq', 'Wk', 'bk', 'Wv', 'bv', 'We', 'Wskip', 'bskip')}
    del _L0_gnn_all

    def _L1_gnn_setup():
        import jax, jax.numpy as jnp
        import numpy as np
        N_NODES = 12500
        N_INCID = 250000
        HIDDEN = 128
        N_HE = 12500
        key = jax.random.key(seed)
        k1, k2, k3 = jax.random.split(key, 3)
        node_feats = jax.random.normal(k1, (N_NODES, HIDDEN), dtype=jnp.float32)
        hyperedge_index = jax.random.randint(k2, (2, N_INCID), 0, N_HE, dtype=jnp.int64)
        bound = float(np.sqrt(6.0 / (HIDDEN + 1)))
        W = jax.random.uniform(k3, (1, HIDDEN), dtype=jnp.float32, minval=-bound, maxval=bound)
        return {'node_feats': node_feats, 'hyperedge_index': hyperedge_index, 'num_hyperedges': N_HE, 'W': W}
    _L1_gnn_all = _L1_gnn_setup()
    _L1_gnn_in = {k: v for k, v in _L1_gnn_all.items() if k in ('W',)}
    del _L1_gnn_all
    return {'x': x, 'src': src, 'dst': dst, 'edge_attr_64': edge_attr_64, 'edge_weight': edge_weight, 'node_vec': node_vec, 'L0_gnn_time_w': _L0_gnn_in['time_w'], 'L0_gnn_time_b': _L0_gnn_in['time_b'], 'L0_gnn_Wq': _L0_gnn_in['Wq'], 'L0_gnn_bq': _L0_gnn_in['bq'], 'L0_gnn_Wk': _L0_gnn_in['Wk'], 'L0_gnn_bk': _L0_gnn_in['bk'], 'L0_gnn_Wv': _L0_gnn_in['Wv'], 'L0_gnn_bv': _L0_gnn_in['bv'], 'L0_gnn_We': _L0_gnn_in['We'], 'L0_gnn_Wskip': _L0_gnn_in['Wskip'], 'L0_gnn_bskip': _L0_gnn_in['bskip'], 'L1_gnn_W': _L1_gnn_in['W']}

def reference(x, src, dst, edge_attr_64, edge_weight, node_vec, L0_gnn_time_w, L0_gnn_time_b, L0_gnn_Wq, L0_gnn_bq, L0_gnn_Wk, L0_gnn_bk, L0_gnn_Wv, L0_gnn_bv, L0_gnn_We, L0_gnn_Wskip, L0_gnn_bskip, L1_gnn_W):
    import jax
    import jax.numpy as jnp

    def _L0_gnn_ref(x, last_update, t, msg, edge_index, time_w, time_b, Wq, bq, Wk, bk, Wv, bv, We, Wskip, bskip):
        import jax, jax.numpy as jnp
        import numpy as np
        import math
        N = 12500
        E = 100000
        IN = 128
        OUT = 128
        MSG = 64
        TDIM = 32
        HEADS = 2
        CH = OUT // HEADS
        EDGE_DIM = MSG + TDIM
        src = edge_index[0]
        dst = edge_index[1]
        rel_t = last_update[src] - t
        rel_t_enc = jnp.cos(rel_t[:, None] * time_w[None, :] + time_b)
        edge_attr = jnp.concatenate([rel_t_enc, msg], axis=-1)
        q_all = x @ Wq + bq
        k_all = x @ Wk + bk
        v_all = x @ Wv + bv
        q = q_all[dst].reshape(-1, HEADS, CH)
        k = k_all[src].reshape(-1, HEADS, CH)
        v = v_all[src].reshape(-1, HEADS, CH)
        e = (edge_attr @ We).reshape(-1, HEADS, CH)
        k = k + e
        alpha = jnp.sum(q * k, axis=-1) / math.sqrt(CH)
        m = jax.ops.segment_max(alpha, dst, num_segments=N)
        m = jnp.where(jnp.isfinite(m), m, 0.0)
        ex = jnp.exp(alpha - m[dst])
        denom = jax.ops.segment_sum(ex, dst, num_segments=N)
        a = ex / (denom[dst] + 1e-16)
        out_e = (v + e) * a[:, :, None]
        out = jax.ops.segment_sum(out_e.reshape(-1, HEADS * CH), dst, num_segments=N)
        out = out + x @ Wskip + bskip
        return out

    def _L1_gnn_ref(node_feats, hyperedge_index, num_hyperedges, W):
        import jax, jax.numpy as jnp
        import numpy as np
        N_NODES = 12500
        N_INCID = 250000
        HIDDEN = 128
        N_HE = 12500
        node_idx = hyperedge_index[0]
        he_idx = hyperedge_index[1]
        gathered = node_feats[node_idx]
        scores = jnp.einsum('ed,d->e', gathered, W[0])
        seg_max = jax.ops.segment_max(scores, he_idx, num_segments=num_hyperedges)
        seg_max = jnp.where(jnp.isfinite(seg_max), seg_max, 0.0)
        w = jnp.exp(scores - seg_max[he_idx])
        denom = jax.ops.segment_sum(w, he_idx, num_segments=num_hyperedges)
        w_norm = w / jnp.maximum(denom, 1e-20)[he_idx]
        out = jax.ops.segment_sum(w_norm[:, None] * gathered, he_idx, num_segments=num_hyperedges)
        return out
    edge_index = jnp.stack([src, dst])
    h = jnp.maximum(_layernorm(x, axis=-1), 0.0)
    x = x + _L0_gnn_ref(h, node_vec, edge_weight, edge_attr_64, edge_index, L0_gnn_time_w, L0_gnn_time_b, L0_gnn_Wq, L0_gnn_bq, L0_gnn_Wk, L0_gnn_bk, L0_gnn_Wv, L0_gnn_bv, L0_gnn_We, L0_gnn_Wskip, L0_gnn_bskip)
    h = jnp.maximum(_layernorm(x, axis=-1), 0.0)
    x = x + _L1_gnn_ref(h, edge_index, 12500, L1_gnn_W)
    return x

_drawn_inputs = setup_inputs


def setup_inputs(seed=0):
    import zlib

    import numpy as np

    out = dict(_drawn_inputs(seed))
    spreads = {'L0_gnn_bq': (0.0, 0.353),
     'L0_gnn_bk': (0.0, 0.8),
     'L0_gnn_bv': (0.0, 0.1),
     'L0_gnn_bskip': (0.0, 0.1)}
    factors = {'L0_gnn_time_b': 4.159}
    for name, (base, spread) in spreads.items():
        noise = np.random.default_rng([zlib.crc32(name.encode()), seed]).standard_normal(out[name].shape)
        drawn = base * np.exp(spread * noise) if base else spread * noise
        out[name] = jnp.asarray(drawn.astype(out[name].dtype))
    for name, factor in factors.items():
        out[name] = (out[name] * factor).astype(out[name].dtype)
    return out
```

```python
from contextlib import ExitStack

import numpy as np

import concourse.bass as bass
from concourse import mybir
from concourse.alu_op_type import AluOpType as ALU

F32 = mybir.dt.float32
BF16 = mybir.dt.bfloat16
I32 = mybir.dt.int32
ACT = mybir.ActivationFunctionType
AX = mybir.AxisListType

P = 128
SUBS = 2
TILE = SUBS * P
STEPS = 8
G = STEPS * SUBS
BLOCK_OPS = 10
GROUP = 4
BIG = 1.0e30
MAGIC = 12582912.0
TWO_PI_HI = 6.28125
TWO_PI_LO = float(2 * np.pi - 6.28125)
PI_BELOW = 3.1415925
EPS = 1e-5


class Chunk:

    def __init__(self, number, half, parity, early=False):
        self.number, self.half, self.parity, self.early = number, half, parity, early


class Chain:

    def __init__(self, engine, semaphore):
        self.engine, self.semaphore, self.base, self.count = engine, semaphore, 0, 0

    def ran(self, instruction):
        instruction.then_inc(self.semaphore, 1)
        self.count += 1

    def settle(self):
        self.engine.wait_ge(self.semaphore, self.base + self.count)

    def loop(self, index, start, per):
        self.base, self.count = index * per + start, 0


def over_chunks(engine, chunks, chain, body, tail=None):
    body(Chunk(0, 0, 0, True), None)
    before = chain.count if chain else 0
    body(Chunk(1, 0, 1, True), Chunk(0, 0, 0))
    if chain:
        per = chain.count - before
        outer, start = chain.base, chain.count
    with engine.Fori(0, (chunks - 2) // 2) as i:
        if chain:
            chain.loop(i, outer + start, 2 * per)
        body(Chunk(i * 2 + 2, i + 1, 0), Chunk(i * 2 + 1, i, 1))
        body(Chunk(i * 2 + 3, i + 1, 1), Chunk(i * 2 + 2, i + 1, 0))
        if chain:
            assert chain.count == 2 * per
    if chain:
        chain.base, chain.count = outer + start + (chunks - 2) * per, 0
    if tail:
        tail(Chunk(chunks - 1, (chunks - 1) // 2, (chunks - 1) % 2))


def registers(nc, engine, row, top):
    return nc.values_load_multi_w_load_instructions(
        row, engines=[engine], min_val=0, max_val=top,
        skip_runtime_bounds_check_because="they are counted on the chip, within the table by construction")[1]


class LayerSemaphores:

    def __init__(self, sem, layer):
        def one(name):
            return sem(f"{name}_{layer}")

        def two(name):
            return [sem(f"{name}_{layer}_{u}") for u in range(2)]

        self.idx_in, self.rows_in = two("idx_in"), two("rows_in")
        self.e_in, self.p_in = two("edge_data_in"), two("tables_in")
        self.sums_stored = two("sums_stored")
        self.angle_turned, self.e_ready = one("angle_turned"), one("e_and_q_ready")
        self.alpha_turned, self.scan_turned = one("alpha_turned"), one("scan_turned")
        self.z_summed, self.m_spread, self.part_ready = one("z_summed"), one("m_spread"), one("part_ready")
        self.angle_ready, self.angle_reduced = one("angle_ready"), one("angle_reduced")
        self.oh_t_ready, self.e_read, self.alpha_ready = one("one_hot_t_ready"), one("e_and_q_read"), one("alpha_ready")
        self.scanned, self.z_ready, self.m_ready = one("scanned"), one("z_ready"), one("m_ready")
        self.decay_ready, self.shift_ready = one("decay_ready"), one("shift_ready")
        self.weighted_ready, self.part_read = one("weighted_ready"), one("part_read")
        self.turns_ready, self.time_ready = one("turns_ready"), one("time_ready")
        self.decay_in, self.p_ready = one("decay_in"), one("p_ready")


def build(nc, heads_0, x, src_rows, dst_rows, t_rows, tile_last, msg_t, node_vec, time_w, time_b, w_all, b_all,
          w_edge, w_score, out):
    n_pad, D = x.shape
    HEADS = heads_0
    CH = D // HEADS
    TDIM = time_w.shape[1]
    MSG = msg_t.shape[1] // SUBS
    windows, tiles = n_pad // P, tile_last.shape[1]
    tile_rows = src_rows.shape[0]
    blocks = tile_rows // P - 1
    chunks = -(-(tiles + windows - 1) // STEPS)
    chunks += chunks % 2
    assert windows % 2 == 0 and windows >= 4 and chunks >= 4 and chunks * STEPS <= blocks * P
    NB = blocks * P
    CPB = P // STEPS
    NQ = G // GROUP
    W0 = HEADS * (CH + 1)
    W1 = D + 1
    SCALE = float(CH) ** -0.5
    KV = 2 * D + 1
    HT = D + 2
    TAB = 3 * G + STEPS
    assert TDIM * GROUP == P and MSG * SUBS == P and windows <= P

    def dram(name, shape, dtype):
        return nc.dram_tensor(name, shape, dtype, kind="Internal").ap()

    idx_dram = dram("idx_by_chunk", [blocks * CPB, P, G], I32)
    t_dram = dram("t_by_chunk", [blocks * CPB, P, G], F32)
    tab_dram = dram("tab_by_chunk", [blocks * CPB, P, TAB], F32)
    rel_dram = dram("rel_by_step", [NB, TILE], BF16)
    start_dram = dram("segment_start_by_sub", [NB * SUBS, HEADS, P], F32)
    sched_dram = dram("tile_and_window_of_step", [2, NB], I32)
    last_dram = dram("last_step_of_window", [P, 1], I32)
    kv_dram = dram("k_v_time_by_node", [n_pad, KV], F32)
    base_dram = dram("x_plus_skip", [n_pad, D], F32)
    h_dram = dram("h_one_score_by_node", [n_pad, HT], F32)
    sums_dram = dram("sums_by_step", [NB, P, W0], F32)
    x1_dram = dram("x_after_layer_0", [n_pad, D], F32)

    with ExitStack() as ctx:
        def sb(name, shape, dtype=F32):
            return ctx.enter_context(nc.sbuf_tensor(name, shape, dtype))

        def ps(name):
            return ctx.enter_context(nc.psum_tensor(name, [P, 512], F32))

        def sem(name):
            return ctx.enter_context(nc.semaphore(name))

        iota_p = sb("iota_p", [P, 1])
        iota_row = sb("iota_row", [P, P])
        ident = sb("ident", [P, P])
        ones = sb("ones", [P, P])
        w_in = sb("w_in", [P, 4 * D])
        b_in = sb("b_in", [P, 4 * D])
        w_e_time = sb("w_e_time", [P, GROUP * D])
        w_e_msg = sb("w_e_msg", [P, SUBS * D])
        time_row = sb("time_row", [P, TDIM])
        time_bias = sb("time_bias", [P, 1])
        time_shift = sb("time_shift", [P, 1])
        magic = sb("magic", [P, 1])
        node_time = sb("node_time", [P, windows])
        node_s = [sb(f"node_s{u}", [P, 8]) for u in range(2)]
        stats = [sb(f"stats{u}", [P, 6]) for u in range(2)]
        score_row = sb("score_row", [P, D])
        q_parts = sb("q_parts", [P, windows * 3 * D], BF16)
        idx = [sb(f"idx{u}", [P, G], I32) for u in range(2)]
        kv = [sb(f"kv{u}", [P, G, KV]) for u in range(2)]
        msg = [sb(f"msg{u}", [P, STEPS, P]) for u in range(2)]
        t_in = [sb(f"t_in{u}", [P, G]) for u in range(2)]
        rel_b = [sb(f"rel_b{u}", [P, G * P], BF16) for u in range(2)]
        tab = [sb(f"tab{u}", [P, TAB]) for u in range(2)]
        start_b = [sb(f"start_b{u}", [G * HEADS, P]) for u in range(2)]
        oh_t = [sb(f"one_hot_t{u}", [P, G * P], BF16) for u in range(2)]
        ve = [sb(f"ve{u}", [P, G, D]) for u in range(2)]
        alpha = [sb(f"alpha{u}", [P, G, HEADS]) for u in range(2)]
        m_run = [sb(f"m_run{u}", [P, HEADS, STEPS + 1]) for u in range(2)]
        sums = [sb(f"sums{u}", [P, STEPS + 1, W0]) for u in range(2)]
        oh = sb("one_hot", [P, G, P])
        pv = sb("weighted", [P, G, HEADS, CH + 1])
        rel_t = sb("rel_t", [P, G])
        ang = sb("angle", [P, G * TDIM])
        ang_u = sb("angle_u", [P, G * TDIM])
        ang_k = sb("angle_k", [P, G * TDIM])
        te = sb("time_code", [P, NQ, P])
        prod = sb("prod", [P, GROUP, D])
        ke = sb("ke", [P, GROUP, D])
        seg = sb("seg_max", [P, P])
        z = sb("z", [P, G, HEADS + 1])
        zs = sb("z_by_node", [P, G, HEADS + 1])
        absent = sb("absent", [P, G])
        m_step = sb("m_step", [P, HEADS, STEPS])
        m_parts = sb("m_parts", [P, STEPS, 3, HEADS], BF16)
        m_rest = sb("m_rest", [P, STEPS, HEADS])
        decay = sb("decay", [P, STEPS, HEADS])
        shifted = sb("shifted", [P, G, HEADS])
        p_col = sb("p_col", [P, G])

        bank = [ps(f"bank{i}") for i in range(8)]
        e_bank, q_bank, x_bank, part_bank, m_bank = bank[0:2], bank[2:4], bank[4], bank[5:7], bank[7]
        MB_BACK, MB_Z, MB_M = P, 2 * P, 2 * P + G * (HEADS + 1)

        vector_chain, scalar_chain = sem("vector_chain"), sem("scalar_chain")
        constants_loaded, iotas_written = sem("constants_loaded"), sem("iotas_written")
        blocks_clear = sem("blocks_clear")
        gather_apart, vector_apart, sync_apart = sem("gather_apart"), sem("vector_apart"), sem("sync_apart")
        merge_ready, merge_summed, merge_turned = sem("merge_ready"), sem("merge_summed"), sem("merge_turned")
        sched_ready, sched_stored = sem("sched_ready"), sem("sched_stored")
        idx_col_ready, block_idx_ready = sem("idx_col_ready"), sem("block_idx_ready")
        rows_gathered, rows_decoded, block_turned = sem("rows_gathered"), sem("rows_decoded"), sem("block_turned")
        block_ready, block_stored = sem("block_ready"), sem("block_stored")
        x_loaded = [sem(f"x_loaded{u}") for u in range(2)]
        h_ready, h_turned, h_copied = sem("h_ready"), sem("h_turned"), sem("h_copied")
        var_ready, std_ready = sem("var_ready"), sem("std_ready")
        proj_ready, node_ready = sem("proj_ready"), sem("node_ready")
        node_stored = [sem(f"node_stored{u}") for u in range(2)]
        fin_loaded = [sem(f"fin_loaded{u}") for u in range(2)]
        fin_var_ready, fin_std_ready, fin_ready = sem("fin_var_ready"), sem("fin_std_ready"), sem("fin_ready")
        fin_stored = [sem(f"fin_stored{u}") for u in range(2)]
        out_loaded = [sem(f"out_loaded{u}") for u in range(2)]
        out_ready = sem("out_ready")
        out_stored = [sem(f"out_stored{u}") for u in range(2)]
        L = [LayerSemaphores(sem, layer) for layer in range(2)]

        pv_flat = pv[:].rearrange("p g h d -> p (g h d)")
        oh_flat = oh[:].rearrange("p g n -> p (g n)")
        kv_out = [pv_flat[:, u * (KV + 3):u * (KV + 3) + KV] for u in range(2)]
        fin_h = [pv_flat[:, u * (KV + 3):u * (KV + 3) + HT] for u in range(2)]
        proj = [oh_flat[:, u * 4 * D:(u + 1) * 4 * D] for u in range(2)]
        early = kv[0][:].rearrange("p a b -> p (a b)")
        late = kv[1][:].rearrange("p a b -> p (a b)")
        tile_last_b = early[:, 0:tiles].bitcast(I32)
        below = early[:, tiles:2 * tiles]
        passed = early[:, 2 * tiles:2 * tiles + NB]
        iota_s = early[:, 2 * tiles + NB:2 * tiles + 2 * NB]
        ve0 = ve[0][:].rearrange("p a b -> p (a b)")
        ve1 = ve[1][:].rearrange("p a b -> p (a b)")
        win = ve0[:, 0:NB]
        reset = ve0[:, NB:2 * NB]
        sched_i = ve1[:, 0:NB].bitcast(I32)
        sched_w = ve1[:, NB:2 * NB].bitcast(I32)
        merge_c = sb("merge_c", [P, 2])
        last_i = sb("last_i", [P, 1], I32)
        win_col = sb("win_col", [P, blocks])
        tile_col = sb("tile_col", [P, blocks], I32)
        iota_k = sb("iota_k", [P, blocks])
        tile_idx = sb("tile_idx", [P, 1], I32)
        take = lambda at, n: late[:, at:at + n]
        src_r, dst_r = take(0, TILE).bitcast(I32), take(TILE, TILE).bitcast(I32)
        t_r, src_f, rel_f = take(2 * TILE, TILE), take(3 * TILE, TILE), take(4 * TILE, TILE)
        begins, ends = take(5 * TILE, TILE), take(6 * TILE, TILE)
        rel_h = take(7 * TILE, P).bitcast(BF16)
        room = 7 * TILE + P
        idx_b = take(room, CPB * G).bitcast(I32)
        t_b = take(room + CPB * G, CPB * G)
        tab_b = take(room + 2 * CPB * G, CPB * TAB).rearrange("p (c f) -> p c f", c=CPB)

        def alpha_2d(u, heads):
            return alpha[u][:].rearrange("p g h -> p (g h)") if heads == HEADS else alpha[u][:, :, 0]

        def z_all(heads):
            return z[:, :, 0:heads + 1]

        def z_view(g, heads):
            return z[:, g, 0:heads + 1]

        def zs_all(heads):
            return zs[:, :, 0:heads + 1]

        def m_parts_view(step, heads):
            return m_parts[:, step, :, 0:heads].rearrange("p n h -> p (n h)") if heads == HEADS else m_parts[:, step, :, 0]

        block = ctx.enter_context(nc.Block())

        @block.gpsimd
        def _(pool):
            pool.iota(iota_p[:], [[0, 1]], base=0, channel_multiplier=1,
                      allow_small_or_imprecise_dtypes=True).then_inc(iotas_written, 1)
            pool.iota(iota_row[:], [[1, P]], base=0, channel_multiplier=0,
                      allow_small_or_imprecise_dtypes=True).then_inc(iotas_written, 1)
            pool.iota(iota_s, [[1, NB]], base=0, channel_multiplier=0,
                      allow_small_or_imprecise_dtypes=True).then_inc(iotas_written, 1)
            pool.iota(iota_k[:], [[P, blocks]], base=0, channel_multiplier=1,
                      allow_small_or_imprecise_dtypes=True).then_inc(iotas_written, 1)

            with pool.Fori(0, blocks) as k:
                pool.wait_ge(block_idx_ready, k + 1)
                pool.sem_inc(gather_apart, 1)
                for rows, table in ((src_r, src_rows), (dst_r, dst_rows), (t_r, t_rows)):
                    pool.indirect_dma_start(rows, None, table, bass.IndirectOffsetOnAxis(ap=tile_idx[:, 0:1], axis=0)
                                            ).then_inc(rows_gathered, 16)
                pool.wait_ge(rows_gathered, k * 48 + 48)

            def gather(s, c, table, width):
                pool.wait_ge(s.idx_in[c.parity], c.half * 16 + 16)
                pool.sem_inc(gather_apart, 1)
                rows = kv[c.parity][:].rearrange("p a b -> p (a b)")
                for g in range(G):
                    pool.indirect_dma_start(rows[:, g * width:(g + 1) * width], None, table,
                                            bass.IndirectOffsetOnAxis(ap=idx[c.parity][:, g:g + 1], axis=0)
                                            ).then_inc(s.rows_in[c.parity], 16)

            def layer_0(c, before):
                if not c.early:
                    pool.wait_ge(L[0].alpha_ready, before.number)
                gather(L[0], c, kv_dram, KV)

            over_chunks(pool, chunks, None, layer_0)

            def layer_1(c, before):
                if not c.early:
                    pool.wait_ge(L[1].part_ready, before.number * STEPS)
                gather(L[1], c, h_dram, HT)

            over_chunks(pool, chunks, None, layer_1)

        @block.sync
        def _(sp):
            for dst, src in ((w_in[:], w_all), (b_in[:], b_all.broadcast_to([P, 4 * D])), (time_row[:], time_w.broadcast_to([P, TDIM])), (score_row[:], w_score.broadcast_to([P, D])),
                             (node_time[:], node_vec), (tile_last_b, tile_last.broadcast_to([P, tiles]))):
                sp.dma_start(dst, src).then_inc(constants_loaded, 16)
            sp.wait_ge(blocks_clear, 2)
            for b in range(SUBS):
                sp.dma_start(w_e_msg[b * MSG:(b + 1) * MSG, b * D:(b + 1) * D], w_edge[TDIM:TDIM + MSG, :]
                             ).then_inc(constants_loaded, 16)
            for b in range(GROUP):
                sp.dma_start(w_e_time[b * TDIM:(b + 1) * TDIM, b * D:(b + 1) * D], w_edge[0:TDIM, :]
                             ).then_inc(constants_loaded, 16)
                sp.dma_start(time_bias[b * TDIM:(b + 1) * TDIM, :], time_b).then_inc(constants_loaded, 16)

            sp.wait_ge(sched_ready, 1)
            sp.dma_start(sched_dram[0:1, :], sched_i[0:1, :]).then_inc(sched_stored, 16)
            sp.dma_start(sched_dram[1:2, :], sched_w[0:1, :]).then_inc(sched_stored, 16)
            sp.dma_start(last_dram, last_i[:]).then_inc(sched_stored, 16)
            with sp.Fori(0, blocks) as k:
                sp.wait_ge(block_ready, k + 1)
                chunk = bass.ds(k * CPB, CPB)
                sp.dma_start(idx_dram[chunk].rearrange("c e f -> e c f"), idx_b.rearrange("p (c f) -> p c f", c=CPB)
                             ).then_inc(block_stored, 16)
                sp.dma_start(t_dram[chunk].rearrange("c e f -> e c f"), t_b.rearrange("p (c f) -> p c f", c=CPB)
                             ).then_inc(block_stored, 16)
                sp.dma_start(tab_dram[chunk].rearrange("c e f -> e c f"), tab_b).then_inc(block_stored, 16)
                sp.dma_start(rel_dram[bass.ds(k * P, P)], rel_h).then_inc(block_stored, 16)
                for h in range(HEADS):
                    sp.dma_start(start_dram.rearrange("(s b) h e -> s b h e", b=SUBS)[bass.ds(k * P, P), :, h, :],
                                 begins.rearrange("p (b e) -> p b e", b=SUBS)).then_inc(block_stored, 16)

            def node_tile(c, before):
                u = c.parity
                if not c.early:
                    sp.wait_ge(node_stored[u], c.half * 32)
                rows = bass.ds(c.number * P, P)
                sp.dma_start(msg[u][:, 0, :], x[rows]).then_inc(x_loaded[u], 16)
                if before is not None:
                    store_node(before)

            def store_node(c):
                u = c.parity
                rows = bass.ds(c.number * P, P)
                sp.wait_ge(node_ready, c.number + 1)
                sp.dma_start(kv_dram[rows], kv_out[u]).then_inc(node_stored[u], 16)
                sp.dma_start(base_dram[rows], msg[u][:, 3, :]).then_inc(node_stored[u], 16)

            over_chunks(sp, windows, None, node_tile, store_node)
            for u in range(2):
                sp.wait_ge(node_stored[u], windows // 2 * 32)
            sp.wait_ge(block_stored, blocks * 96)
            sp.wait_ge(sched_stored, 48)

            def load_idx(s, c, before):
                if not c.early:
                    sp.wait_ge(s.rows_in[c.parity], c.half * 16 * G)
                sp.dma_start(idx[c.parity][:], idx_dram[bass.ds(c.number, 1)].rearrange("c e f -> (c e) f")
                             ).then_inc(s.idx_in[c.parity], 16)

            def load_rel(s, c):
                row = rel_dram[bass.ds(c.number * STEPS, STEPS)].rearrange("(o s) e -> o (s e)", o=1)
                sp.dma_start(rel_b[c.parity][:], row.broadcast_to([P, G * P])).then_inc(s.e_in[c.parity], 16)

            def load_tab(s, c, heads):
                rows = start_dram[bass.ds(c.number * G, G), 0:heads, :].rearrange("s h e -> (s h) e") if heads == HEADS \
                    else start_dram[bass.ds(c.number * G, G), 0, :]
                sp.dma_start(tab[c.parity][:], tab_dram[bass.ds(c.number, 1)].rearrange("c e f -> (c e) f")
                             ).then_inc(s.p_in[c.parity], 16)
                sp.dma_start(start_b[c.parity][0:G * heads, :], rows).then_inc(s.p_in[c.parity], 16)

            def store_sums(s, c):
                sp.wait_ge(s.part_read, c.number * STEPS + STEPS)
                sp.dma_start(sums_dram[bass.ds(c.number * STEPS, STEPS)].rearrange("s e f -> e s f"),
                             sums[c.parity][:, 1:STEPS + 1, :]).then_inc(s.sums_stored[c.parity], 16)

            def layer_0(c, before):
                u, s = c.parity, L[0]
                load_idx(s, c, before)
                if not c.early:
                    sp.wait_ge(s.alpha_ready, before.number)
                sp.dma_start(t_in[u][:], t_dram[bass.ds(c.number, 1)].rearrange("c e f -> (c e) f")
                             ).then_inc(s.e_in[u], 16)
                load_rel(s, c)
                sp.sem_inc(sync_apart, 1)
                tile_of = registers(nc, mybir.EngineType.SP, sched_dram[0:1, bass.ds(c.number * STEPS, STEPS)], tile_rows - 1)
                for j in range(STEPS):
                    sp.dma_start(msg[u][:, j, :], msg_t[bass.ds(tile_of[j], 1)].rearrange("t m e -> (t m) e")
                                 ).then_inc(s.e_in[u], 16)
                if not c.early:
                    store_sums(s, Chunk(before.number - 1, None, u))
                load_tab(s, c, HEADS)

            over_chunks(sp, chunks, None, layer_0)
            for c in (chunks - 2, chunks - 1):
                store_sums(L[0], Chunk(c, None, c % 2))
            for u in range(2):
                sp.wait_ge(L[0].sums_stored[u], chunks // 2 * 16)

            def load_sums(c, into, rest, what, freed):
                u = c.parity
                sp.sem_inc(sync_apart, 1)
                step = registers(nc, mybir.EngineType.SP, last_dram[bass.ds(c.number, 1)].rearrange("a b -> b a"), NB - 1)[0]
                sp.dma_start(into, sums_dram[bass.ds(step, 1)].rearrange("s e f -> (s e) f")).then_inc(what[u], 16)
                sp.dma_start(rest, freed[bass.ds(c.number * P, P)]).then_inc(what[u], 16)

            def fin_tile(c, before):
                u = c.parity
                if not c.early:
                    sp.wait_ge(fin_stored[u], c.half * 32)
                load_sums(c, sums[u][:, 1, :], msg[u][:, 0, :], fin_loaded, base_dram)
                if before is not None:
                    store_fin(before)

            def store_fin(c):
                u, rows = c.parity, bass.ds(c.number * P, P)
                sp.wait_ge(fin_ready, c.number + 1)
                sp.dma_start(h_dram[rows], fin_h[u]).then_inc(fin_stored[u], 16)
                sp.dma_start(x1_dram[rows], msg[u][:, 1, :]).then_inc(fin_stored[u], 16)

            over_chunks(sp, windows, None, fin_tile, store_fin)
            for u in range(2):
                sp.wait_ge(fin_stored[u], windows // 2 * 32)

            def layer_1(c, before):
                s = L[1]
                load_idx(s, c, before)
                if not c.early:
                    store_sums(s, Chunk(before.number - 1, None, c.parity))
                load_rel(s, c)
                load_tab(s, c, 1)

            over_chunks(sp, chunks, None, layer_1)
            for c in (chunks - 2, chunks - 1):
                store_sums(L[1], Chunk(c, None, c % 2))
            for u in range(2):
                sp.wait_ge(L[1].sums_stored[u], chunks // 2 * 16)

            def out_tile(c, before):
                u = c.parity
                if not c.early:
                    sp.wait_ge(out_stored[u], c.half * 16)
                load_sums(c, sums[u][:, 1, :], msg[u][:, 0, :], out_loaded, x1_dram)
                if before is not None:
                    store_out(before)

            def store_out(c):
                u = c.parity
                sp.wait_ge(out_ready, c.number + 1)
                sp.dma_start(out[bass.ds(c.number * P, P)], msg[u][:, 1, :]).then_inc(out_stored[u], 16)

            over_chunks(sp, windows, None, out_tile, store_out)
            for u in range(2):
                sp.wait_ge(out_stored[u], windows // 2 * 16)

        @block.scalar
        def _(act):
            chain = Chain(act, scalar_chain)

            def node_tile(c, before):
                u = c.parity
                act.wait_ge(var_ready, c.number + 1)
                act.activation(node_s[u][:, 3:4], node_s[u][:, 2:3], ACT.Sqrt).then_inc(std_ready, 1)
                act.wait_ge(h_turned, c.number + 1)
                if not c.early:
                    act.wait_ge(proj_ready, before.number)
                act.activation(msg[u][:, 2, :], bank[u][:, 0:P], ACT.Relu).then_inc(h_copied, 1)

            over_chunks(act, windows, None, node_tile)


            def exp_decay(s, c, heads):
                act.wait_ge(s.decay_ready, c.number + 1)
                act.activation(decay[:, :, 0:heads], decay[:, :, 0:heads], ACT.Exp).then_inc(s.decay_in, 1)


            def layer_0(c, before):
                s = L[0]
                act.wait_ge(s.angle_turned, c.number + 1)
                if before is not None:
                    act.wait_ge(s.angle_reduced, c.number)
                chain.ran(act.activation(ang_u[:], x_bank[:], ACT.Identity, bias=time_shift[:, 0:1]))
                chain.settle()
                act.activation(ang_k[:], ang_u[:], ACT.Identity, bias=magic[:, 0:1], scale=float(1 / (2 * np.pi))
                               ).then_inc(s.turns_ready, 1)
                act.wait_ge(s.angle_reduced, c.number + 1)
                if before is not None:
                    act.wait_ge(s.e_ready, c.number * NQ)
                act.activation(te[:].rearrange("p q e -> p (q e)"), ang[:], ACT.Sin).then_inc(s.time_ready, 1)
                if before is not None:
                    weights_0(before)

            def weights_0(c):
                s = L[0]
                exp_decay(s, c, HEADS)
                act.wait_ge(s.shift_ready, c.number + 1)
                act.activation(pv[:, :, :, CH], shifted[:], ACT.Exp).then_inc(s.p_ready, 1)

            over_chunks(act, chunks, chain, layer_0, weights_0)

            def fin_tile(c, before):
                act.wait_ge(fin_var_ready, c.number + 1)
                act.activation(node_s[c.parity][:, 3:4], node_s[c.parity][:, 2:3], ACT.Sqrt).then_inc(fin_std_ready, 1)

            over_chunks(act, windows, None, fin_tile)

            def layer_1(c, before):
                s = L[1]
                exp_decay(s, c, 1)
                act.wait_ge(s.shift_ready, c.number + 1)
                act.activation(p_col[:], shifted[:, :, 0], ACT.Exp).then_inc(s.p_ready, 1)

            over_chunks(act, chunks, None, layer_1)

        @block.tensor
        def _(pe):
            pe.wait_ge(merge_ready, 1)
            for half in range(2):
                mm = pe.matmul(part_bank[half][:, 0:NB // 2], ones[0:windows - 1, :],
                               passed[0:windows - 1, half * (NB // 2):(half + 1) * (NB // 2)], start=True, stop=True)
            for k in range(blocks):
                mm = pe.matmul(m_bank[:, k:k + 1], passed[0:windows - 1, k * P:(k + 1) * P], ones[0:windows - 1, 0:1],
                               start=True, stop=True)
            mm.then_inc(merge_summed, 1)

            with pe.Fori(0, blocks) as k:
                pe.wait_ge(rows_decoded, k + 1)
                for n, rows in enumerate((src_f, rel_f, t_r, ends)):
                    for b in range(SUBS):
                        mm = pe.transpose(part_bank[n // 2][:, (n % 2 * SUBS + b) * P:(n % 2 * SUBS + b + 1) * P],
                                          rows[:, b * P:(b + 1) * P], ident[:])
                mm.then_inc(block_turned, 1)

            pe.wait_ge(constants_loaded, 256)

            def node_tile(c, before):
                u = c.parity
                pe.wait_ge(h_ready, c.number + 1)
                if not c.early:
                    pe.wait_ge(h_copied, before.number)
                pe.transpose(bank[u][:, 0:P], msg[u][:, 1, :], ident[:]).then_inc(h_turned, 1)
                pe.wait_ge(h_copied, c.number + 1)
                if not c.early:
                    pe.wait_ge(node_ready, before.number)
                pe.matmul(bank[2 + u][:], msg[u][:, 2, :], w_in[:], start=True, stop=True).then_inc(proj_ready, 1)

            over_chunks(pe, windows, None, node_tile)

            def turn_angles(c, before):
                s = L[0]
                pe.wait_ge(s.angle_ready, c.number + 1)
                if before is not None:
                    pe.wait_ge(s.turns_ready, c.number)
                for q in range(NQ):
                    mm = pe.transpose(x_bank[:, q * P:(q + 1) * P], ang[:, q * P:(q + 1) * P], ident[:])
                mm.then_inc(s.angle_turned, 1)

            def edge_group(c, q, win_of):
                u, s = c.parity, L[0]
                eb, qb = e_bank[q % 2], q_bank[q % 2]
                if not (c.early and c.number == 0 and q < 2):
                    pe.wait_ge(s.e_read, c.number * NQ + q - 1)
                for j in range(GROUP // SUBS):
                    cols = slice(j * SUBS * D, (j + 1) * SUBS * D)
                    pe.matmul(eb[:, cols], te[:, q, :], w_e_time[:, cols], start=True, stop=False)
                    pe.matmul(eb[:, cols], msg[u][:, q * (GROUP // SUBS) + j, :], w_e_msg[:], start=False, stop=True)
                for b in range(GROUP):
                    g = GROUP * q + b
                    for n in range(3):
                        mm = pe.matmul(qb[:, b * D:(b + 1) * D], oh_t[u][:, g * P:(g + 1) * P],
                                       q_parts[:, bass.ds(win_of[g // SUBS] * (3 * D) + n * D, D)],
                                       start=(n == 0), stop=(n == 2))
                mm.then_inc(s.e_ready, 1)

            def turn_alpha(s, c, heads):
                pe.wait_ge(s.alpha_ready, c.number + 1)
                pe.transpose(m_bank[0:G * heads, 0:P], alpha_2d(c.parity, heads), ident[:]).then_inc(s.alpha_turned, 1)

            def turn_scan(s, c, heads):
                pe.wait_ge(s.scanned, c.number + 1)
                pe.transpose(m_bank[:, MB_BACK:MB_BACK + P], seg[:], ident[:]).then_inc(s.scan_turned, 1)

            def sum_z(s, c, heads):
                pe.wait_ge(s.z_ready, c.number + 1)
                n = heads + 1
                for g in range(G):
                    mm = pe.matmul(m_bank[:, MB_Z + g * n:MB_Z + (g + 1) * n], oh[:, g, :], z_view(g, heads),
                                   start=True, stop=True)
                mm.then_inc(s.z_summed, 1)

            def spread_m(s, c, heads):
                pe.wait_ge(s.m_ready, c.number + 1)
                n = 3 * heads
                for g in range(G):
                    mm = pe.matmul(m_bank[:, MB_M + g * n:MB_M + (g + 1) * n], oh_t[c.parity][:, g * P:(g + 1) * P],
                                   m_parts_view(g // SUBS, heads), start=True, stop=True)
                mm.then_inc(s.m_spread, 1)

            def sum_parts(s, c, width, rows):
                for j in range(STEPS):
                    if j % 2 == 0:
                        pe.wait_ge(s.weighted_ready, c.number * NQ + (j // 2 + 1))
                    if not (isinstance(c.number, int) and c.number == 0 and j < 2):
                        pe.wait_ge(s.part_read, c.number * STEPS + (j - 1))
                    for b in range(SUBS):
                        g = SUBS * j + b
                        mm = pe.matmul(part_bank[j % 2][:, 0:width], oh[:, g, :], rows(g),
                                       start=(b == 0), stop=(b == SUBS - 1))
                    mm.then_inc(s.part_ready, 1)

            def weighted_rows(g):
                return pv[:, g, :, :].rearrange("p h d -> p (h d)")

            def layer_0(c, before):
                u, s = c.parity, L[0]
                turn_angles(c, before)
                if before is not None:
                    turn_alpha(s, before, HEADS)
                win_of = registers(nc, mybir.EngineType.PE, sched_dram[1:2, bass.ds(c.number * STEPS, STEPS)], windows - 1)
                pe.wait_ge(s.time_ready, c.number + 1)
                pe.wait_ge(s.oh_t_ready, c.number + 1)
                pe.wait_ge(s.e_in[u], c.half * (16 * (STEPS + 2)) + 16 * (STEPS + 2))
                edge_group(c, 0, win_of)
                if before is not None:
                    turn_scan(s, before, HEADS)
                edge_group(c, 1, win_of)
                if before is not None:
                    sum_z(s, before, HEADS)
                edge_group(c, 2, win_of)
                if before is not None:
                    spread_m(s, before, HEADS)
                edge_group(c, 3, win_of)
                if before is not None:
                    sum_parts(s, before, W0, weighted_rows)

            def last_0(c):
                s = L[0]
                turn_alpha(s, c, HEADS)
                turn_scan(s, c, HEADS)
                sum_z(s, c, HEADS)
                spread_m(s, c, HEADS)
                sum_parts(s, c, W0, weighted_rows)

            pe.wait_ge(sched_stored, 48)
            over_chunks(pe, chunks, None, layer_0, last_0)

            def layer_1(c, before):
                s = L[1]
                turn_alpha(s, c, 1)
                turn_scan(s, c, 1)
                sum_z(s, c, 1)
                spread_m(s, c, 1)
                rows = kv[c.parity][:].rearrange("p a b -> p (a b)")
                sum_parts(s, c, W1, lambda g: rows[:, g * HT:g * HT + W1])

            over_chunks(pe, chunks, None, layer_1)

        @block.vector
        def _(v):
            chain = Chain(v, vector_chain)

            def layernorm(xt, u, var_sem, std_sem, number, hn):
                st, ns = stats[u], node_s[u]
                chain.ran(v.bn_stats(st[:], xt))
                chain.settle()
                v.sem_inc(vector_apart, 1)
                chain.ran(v.bn_aggr(ns[:, 0:2], st[:]))
                chain.settle()
                v.tensor_scalar(ns[:, 2:3], ns[:, 1:2], EPS, None, ALU.add).then_inc(var_sem, 1)
                v.wait_ge(std_sem, number + 1)
                chain.ran(v.reciprocal(ns[:, 4:5], ns[:, 3:4]))
                chain.settle()
                return v.tensor_scalar(hn, xt, ns[:, 0:1], ns[:, 4:5], ALU.subtract, ALU.mult)

            v.memset(w_e_time[:], 0.0).then_inc(blocks_clear, 1)
            v.memset(w_e_msg[:], 0.0).then_inc(blocks_clear, 1)
            v.wait_ge(iotas_written, 4)
            chain.ran(v.tensor_scalar(ident[:], iota_row[:], iota_p[:, 0:1], None, ALU.is_equal))
            chain.ran(v.memset(ones[:], 1.0))
            chain.ran(v.memset(magic[:], MAGIC))
            chain.ran(v.memset(seg[:], 0.0))
            v.wait_ge(constants_loaded, 256)
            chain.ran(v.tensor_scalar(time_shift[:], time_bias[:], float(np.pi / 2), None, ALU.add))
            chain.ran(v.tensor_scalar(merge_c[:, 0:1], iota_p[:], float(P), float(P), ALU.mult, ALU.add))
            chain.settle()
            chain.ran(v.tensor_scalar(below, tile_last_b, merge_c[:, 0:1], None, ALU.is_lt))
            chain.settle()
            chain.ran(v.tensor_reduce(merge_c[:, 1:2], below, AX.X, ALU.add))
            chain.settle()
            chain.ran(v.tensor_tensor(merge_c[:, 0:1], merge_c[:, 1:2], iota_p[:], ALU.add))
            chain.settle()
            chain.ran(v.tensor_scalar(merge_c[:, 1:2], iota_p[:], float(windows - 1), float(chunks * STEPS),
                                      ALU.is_ge, ALU.mult))
            chain.settle()
            chain.ran(v.tensor_scalar(merge_c[:, 1:2], merge_c[:, 1:2], merge_c[:, 0:1], float(chunks * STEPS - 1),
                                      ALU.add, ALU.min))
            chain.settle()
            chain.ran(v.tensor_copy(last_i[:], merge_c[:, 1:2]))
            v.tensor_scalar(passed, iota_s, merge_c[:, 0:1], None, ALU.is_gt).then_inc(merge_ready, 1)
            v.wait_ge(merge_summed, 1)
            for half in range(2):
                cut = slice(half * (NB // 2), (half + 1) * (NB // 2))
                chain.ran(v.tensor_copy(win[:, cut], part_bank[half][:, 0:NB // 2]))
            chain.ran(v.tensor_scalar(win_col[:], m_bank[:, 0:blocks], float(P), None, ALU.mult))
            chain.ran(v.tensor_tensor(tile_col[:], iota_k[:], m_bank[:, 0:blocks], ALU.subtract))
            chain.settle()
            chain.ran(v.tensor_copy(sched_w[0:1, :], win[0:1, :]))
            chain.ran(v.tensor_tensor(reset[:, 1:NB], win[:, 1:NB], win[:, 0:NB - 1], ALU.not_equal))
            chain.ran(v.memset(reset[:, 0:1], 0.0))
            chain.settle()
            chain.ran(v.tensor_scalar(reset, reset, -2.0 * BIG, None, ALU.mult))
            v.tensor_tensor(sched_i[0:1, :], iota_s[0:1, :], win[0:1, :], ALU.subtract).then_inc(sched_ready, 1)
            begins_3, ends_3 = (r.rearrange("p (b e) -> p b e", b=SUBS) for r in (begins, ends))
            rel_3 = rel_f.rearrange("p (b e) -> p b e", b=SUBS)
            chain.ran(v.memset(begins_3[:, :, 0:1], -BIG))
            chain.ran(v.memset(ends_3[:, :, P - 1:P], 1.0))
            chain.settle()

            outer, first = chain.base, chain.count
            with v.Fori(0, blocks) as k:
                chain.loop(k, outer + first, BLOCK_OPS)
                v.tensor_copy(tile_idx[:], tile_col[:, bass.ds(k, 1)]).then_inc(block_idx_ready, 1)
                v.wait_ge(rows_gathered, k * 48 + 48)
                chain.ran(v.tensor_copy(src_f, src_r))
                chain.ran(v.tensor_scalar(rel_f, dst_r, win_col[:, bass.ds(k, 1)], None, ALU.subtract))
                chain.settle()
                chain.ran(v.tensor_scalar(rel_h, rel_f, -1.0, float(P), ALU.max, ALU.min))
                chain.ran(v.tensor_tensor(ends_3[:, :, 0:P - 1], rel_3[:, :, 0:P - 1], rel_3[:, :, 1:P], ALU.not_equal))
                chain.settle()
                v.tensor_scalar(begins_3[:, :, 1:P], ends_3[:, :, 0:P - 1], -BIG, None, ALU.mult).then_inc(rows_decoded, 1)
                v.wait_ge(block_turned, k + 1)

                def turned(n):
                    return part_bank[n // 2][:, n % 2 * TILE:(n % 2 + 1) * TILE].rearrange("p (b c s) -> p c s b", b=SUBS, s=STEPS)

                def column(view, at):
                    return view[:, :, at:at + G].rearrange("p c (s b) -> p c s b", b=SUBS)

                idx_3 = idx_b.rearrange("p (c f) -> p c f", c=CPB)
                t_3 = t_b.rearrange("p (c f) -> p c f", c=CPB)
                chain.ran(v.tensor_copy(column(idx_3, 0), turned(0)))
                chain.ran(v.tensor_copy(column(tab_b, 0), turned(1)))
                chain.ran(v.tensor_copy(column(t_3, 0), turned(2)))
                chain.ran(v.tensor_copy(column(tab_b, G), turned(3)))
                chain.ran(v.tensor_copy(tab_b[:, :, 3 * G:TAB],
                                        reset[:, bass.ds(k * P, P)].rearrange("p (c s) -> p c s", s=STEPS)))
                chain.settle()
                chain.ran(v.tensor_scalar(tab_b[:, :, 2 * G:3 * G], tab_b[:, :, 0:G], 0.0, None, ALU.is_ge))
                chain.settle()
                v.scalar_tensor_tensor(tab_b[:, :, 2 * G:3 * G], tab_b[:, :, 0:G], float(P), tab_b[:, :, 2 * G:3 * G],
                                       ALU.is_lt, ALU.mult).then_inc(block_ready, 1)
                v.wait_ge(block_stored, k * 96 + 96)
                assert chain.count == BLOCK_OPS
            chain.base, chain.count = outer + first + blocks * BLOCK_OPS, 0

            def node_tile(c, before):
                u = c.parity
                xt, hn, base = msg[u][:, 0, :], msg[u][:, 1, :], msg[u][:, 3, :]
                v.wait_ge(x_loaded[u], c.half * 16 + 16)
                layernorm(xt, u, var_ready, std_ready, c.number, hn).then_inc(h_ready, 1)
                v.wait_ge(proj_ready, c.number + 1)
                chain.ran(v.tensor_tensor(proj[u], bank[2 + u][:], b_in[:], ALU.add))
                if not c.early:
                    v.wait_ge(node_stored[u], c.half * 32)
                chain.settle()
                q = proj[u][:, 0:D]
                hi, mid, lo = (q_parts[:, bass.ds(c.number * (3 * D) + n * D, D)] for n in range(3))
                chain.ran(v.tensor_scalar(q, q, SCALE, None, ALU.mult))
                chain.ran(v.tensor_copy(kv_out[u][:, 0:2 * D], proj[u][:, D:3 * D]))
                chain.ran(v.tensor_copy(kv_out[u][:, 2 * D:KV], node_time[:, bass.ds(c.number, 1)]))
                chain.settle()
                chain.ran(v.tensor_copy(hi, q))
                chain.settle()
                chain.ran(v.tensor_tensor(q, q, hi, ALU.subtract))
                chain.settle()
                chain.ran(v.tensor_copy(mid, q))
                chain.settle()
                chain.ran(v.tensor_tensor(lo, q, mid, ALU.subtract))
                v.tensor_tensor(base, xt, proj[u][:, 3 * D:4 * D], ALU.add).then_inc(node_ready, 1)

            over_chunks(v, windows, chain, node_tile)

            def clear_state():
                chain.ran(v.memset(m_run[1][:, :, STEPS:STEPS + 1], -BIG))
                chain.ran(v.memset(sums[1][:, STEPS, :], 0.0))
                chain.settle()

            def one_hot_t(s, c):
                v.tensor_scalar(oh_t[c.parity][:], rel_b[c.parity][:], iota_p[:, 0:1], None, ALU.is_equal
                                ).then_inc(s.oh_t_ready, 1)

            def one_hot(s, c):
                v.wait_ge(s.p_in[c.parity], c.half * 32 + 32)
                for g in range(G):
                    chain.ran(v.tensor_scalar(oh[:, g, :], iota_row[:], tab[c.parity][:, g:g + 1], None, ALU.is_equal))

            def scan(s, c, heads):
                n = G * heads
                v.wait_ge(s.p_in[c.parity], c.half * 32 + 32)
                v.wait_ge(s.alpha_turned, c.number + 1)
                v.tensor_tensor_scan(seg[0:n, :], start_b[c.parity][0:n, :], m_bank[0:n, 0:P], -BIG, ALU.add, ALU.max
                                     ).then_inc(s.scanned, 1)

            def make_z(s, c, heads):
                ends_c = tab[c.parity][:, G:2 * G].unsqueeze(2)
                v.wait_ge(s.scan_turned, c.number + 1)
                back = m_bank[:, MB_BACK:MB_BACK + G * heads].rearrange("p (g h) -> p g h", h=heads)
                chain.ran(v.tensor_tensor(z_all(heads)[:, :, 0:heads], back, ends_c.broadcast_to([P, G, heads]), ALU.mult))
                v.tensor_copy(z_all(heads)[:, :, heads:heads + 1], ends_c).then_inc(s.z_ready, 1)

            def make_m(s, c, heads):
                m, old = m_run[c.parity], m_run[1 - c.parity]
                zn, t = zs_all(heads), tab[c.parity]
                v.wait_ge(s.z_summed, c.number + 1)
                chain.ran(v.tensor_copy(zn, m_bank[:, MB_Z:MB_Z + G * (heads + 1)].rearrange("p (g n) -> p g n", g=G)))
                chain.ran(v.tensor_copy(m[:, 0:heads, 0:1], old[:, 0:heads, STEPS:STEPS + 1]))
                chain.settle()
                chain.ran(v.tensor_scalar(absent[:], zn[:, :, heads], -1.0, BIG, ALU.add, ALU.mult))
                chain.settle()
                chain.ran(v.tensor_tensor(zn[:, :, 0:heads], zn[:, :, 0:heads],
                                          absent[:].unsqueeze(2).broadcast_to([P, G, heads]), ALU.add))
                chain.settle()
                pair = zn.rearrange("p (s b) n -> p b n s", b=SUBS)
                chain.ran(v.tensor_tensor(m_step[:, 0:heads, :], pair[:, 0, 0:heads, :], pair[:, 1, 0:heads, :], ALU.max))
                chain.settle()
                for h in range(heads):
                    chain.ran(v.tensor_tensor_scan(m[:, h, 1:STEPS + 1], t[:, 3 * G:TAB], m_step[:, h, :],
                                                   m[:, h, 0:1], ALU.add, ALU.max))
                chain.settle()
                now = m[:, 0:heads, 1:STEPS + 1].rearrange("p h s -> p s h")
                past = m[:, 0:heads, 0:STEPS].rearrange("p h s -> p s h")
                hi, mid, lo = (m_parts[:, :, n, 0:heads] for n in range(3))
                rest, dec = m_rest[:, :, 0:heads], decay[:, :, 0:heads]
                chain.ran(v.tensor_copy(hi, now))
                chain.ran(v.tensor_tensor(dec, past, t[:, 3 * G:TAB].unsqueeze(2).broadcast_to([P, STEPS, heads]), ALU.add))
                chain.settle()
                chain.ran(v.tensor_tensor(rest, now, hi, ALU.subtract))
                v.tensor_tensor(dec, dec, now, ALU.subtract).then_inc(s.decay_ready, 1)
                chain.settle()
                chain.ran(v.tensor_copy(mid, rest))
                chain.settle()
                v.tensor_tensor(lo, rest, mid, ALU.subtract).then_inc(s.m_ready, 1)

            def shift(s, c, heads):
                v.wait_ge(s.m_spread, c.number + 1)
                spread = m_bank[:, MB_M:MB_M + G * 3 * heads].rearrange("p (g n h) -> p n g h", n=3, h=heads)
                d = shifted[:, :, 0:heads]
                chain.ran(v.tensor_tensor(d, alpha[c.parity][:, :, 0:heads], spread[:, 0], ALU.subtract))
                chain.settle()
                chain.ran(v.tensor_tensor(d, d, spread[:, 1], ALU.subtract))
                chain.settle()
                v.tensor_tensor(d, d, spread[:, 2], ALU.subtract).then_inc(s.shift_ready, 1)

            def add_parts(s, c, heads, width, j):
                S = sums[c.parity]
                if j == 0:
                    v.wait_ge(s.decay_in, c.number + 1)
                    if not c.early:
                        v.wait_ge(s.sums_stored[c.parity], c.half * 16)
                    chain.ran(v.tensor_copy(S[:, 0, :], sums[1 - c.parity][:, STEPS, :]))
                    chain.settle()
                else:
                    v.wait_ge(s.part_read, c.number * STEPS + j)
                v.wait_ge(s.part_ready, c.number * STEPS + (j + 1))
                n = width // heads
                for h in range(heads):
                    last = v.scalar_tensor_tensor(S[:, j + 1, h * n:(h + 1) * n], S[:, j, h * n:(h + 1) * n],
                                                  decay[:, j, h:h + 1], part_bank[j % 2][:, h * n:(h + 1) * n],
                                                  ALU.mult, ALU.add)
                last.then_inc(s.part_read, 1)

            def angles(c, before):
                u, s = c.parity, L[0]
                v.wait_ge(s.rows_in[u], c.half * (16 * G) + 16 * G)
                v.wait_ge(s.e_in[u], c.half * (16 * (STEPS + 2)) + 16 * (STEPS + 2))
                chain.ran(v.tensor_tensor(rel_t[:], kv[u][:, :, 2 * D], t_in[u][:], ALU.subtract))
                chain.settle()
                if before is not None:
                    v.wait_ge(s.time_ready, c.number)
                v.tensor_tensor(ang[:].rearrange("p (g d) -> p g d", g=G),
                                time_row[:].unsqueeze(1).broadcast_to([P, G, TDIM]),
                                rel_t[:].unsqueeze(2).broadcast_to([P, G, TDIM]), ALU.mult).then_inc(s.angle_ready, 1)

            def reduce_angles(c):
                s = L[0]
                v.wait_ge(s.turns_ready, c.number + 1)
                chain.ran(v.tensor_scalar(ang_k[:], ang_k[:], MAGIC, None, ALU.subtract))
                chain.settle()
                chain.ran(v.scalar_tensor_tensor(ang[:], ang_k[:], -TWO_PI_HI, ang_u[:], ALU.mult, ALU.add))
                chain.settle()
                chain.ran(v.scalar_tensor_tensor(ang[:], ang_k[:], -TWO_PI_LO, ang[:], ALU.mult, ALU.add))
                chain.settle()
                v.tensor_scalar(ang[:], ang[:], PI_BELOW, -PI_BELOW, ALU.min, ALU.max).then_inc(s.angle_reduced, 1)

            def score_group(c, q):
                u, s = c.parity, L[0]
                subs = slice(GROUP * q, GROUP * (q + 1))
                e = e_bank[q % 2][:].rearrange("p (g d) -> p g d", g=GROUP)
                qd = q_bank[q % 2][:].rearrange("p (g d) -> p g d", g=GROUP)
                v.wait_ge(s.e_ready, c.number * NQ + (q + 1))
                chain.ran(v.tensor_tensor(ke[:], kv[u][:, subs, 0:D], e, ALU.add))
                chain.ran(v.tensor_tensor(ve[u][:, subs, :], kv[u][:, subs, D:2 * D], e, ALU.add))
                chain.settle()
                v.tensor_tensor(prod[:], ke[:], qd, ALU.mult).then_inc(s.e_read, 1)
                v.wait_ge(s.e_read, c.number * NQ + (q + 1))
                last = v.tensor_reduce(alpha[u][:, subs, :], prod[:].rearrange("p g (h d) -> p g h d", h=HEADS), AX.X, ALU.add)
                if q == NQ - 1:
                    chain.settle()
                    last.then_inc(s.alpha_ready, 1)
                else:
                    chain.ran(last)

            def weigh_group(c, q):
                s = L[0]
                subs = slice(GROUP * q, GROUP * (q + 1))
                v.tensor_tensor(pv[:, subs, :, 0:CH], ve[c.parity][:, subs, :].rearrange("p g (h d) -> p g h d", h=HEADS),
                                pv[:, subs, :, CH:CH + 1].broadcast_to([P, GROUP, HEADS, CH]), ALU.mult
                                ).then_inc(s.weighted_ready, 1)

            def sums_0(c):
                s = L[0]
                v.wait_ge(s.p_ready, c.number + 1)
                weigh_group(c, 0)
                for j in range(STEPS):
                    if j % 2 == 0 and j // 2 + 1 < NQ:
                        weigh_group(c, j // 2 + 1)
                    add_parts(s, c, HEADS, W0, j)

            def layer_0(c, before):
                s = L[0]
                angles(c, before)
                one_hot_t(s, c)
                if before is not None:
                    scan(s, before, HEADS)
                reduce_angles(c)
                if before is not None:
                    one_hot(s, before)
                score_group(c, 0)
                if before is not None:
                    make_z(s, before, HEADS)
                score_group(c, 1)
                if before is not None:
                    make_m(s, before, HEADS)
                score_group(c, 2)
                if before is not None:
                    shift(s, before, HEADS)
                score_group(c, 3)
                if before is not None:
                    sums_0(before)

            def last_0(c):
                s = L[0]
                scan(s, c, HEADS)
                one_hot(s, c)
                make_z(s, c, HEADS)
                make_m(s, c, HEADS)
                shift(s, c, HEADS)
                sums_0(c)

            clear_state()
            over_chunks(v, chunks, chain, layer_0, last_0)

            def fin_tile(c, before):
                u = c.parity
                tot, base, x1, hn, hs = sums[u][:, 1, :], msg[u][:, 0, :], msg[u][:, 1, :], msg[u][:, 2, :], fin_h[u]
                v.wait_ge(fin_loaded[u], c.half * 32 + 32)
                for h in range(HEADS):
                    at = h * (CH + 1) + CH
                    chain.ran(v.tensor_scalar(node_s[u][:, 5 + h:6 + h], tot[:, at:at + 1], 1e-16, None, ALU.add))
                chain.settle()
                chain.ran(v.reciprocal(node_s[u][:, 5:5 + HEADS], node_s[u][:, 5:5 + HEADS]))
                chain.settle()
                for h in range(HEADS):
                    chain.ran(v.scalar_tensor_tensor(x1[:, h * CH:(h + 1) * CH], tot[:, h * (CH + 1):h * (CH + 1) + CH],
                                                     node_s[u][:, 5 + h:6 + h], base[:, h * CH:(h + 1) * CH], ALU.mult, ALU.add))
                chain.settle()
                chain.ran(layernorm(x1, u, fin_var_ready, fin_std_ready, c.number, hn))
                chain.settle()
                chain.ran(v.tensor_scalar(hs[:, 0:D], hn, 0.0, None, ALU.max))
                chain.ran(v.memset(hs[:, D:D + 1], 1.0))
                chain.settle()
                v.tensor_tensor_reduce(hn, hs[:, 0:D], score_row[:], 1.0, 0.0, ALU.mult, ALU.add, hs[:, D + 1:HT]
                                       ).then_inc(fin_ready, 1)

            over_chunks(v, windows, chain, fin_tile)

            def layer_1(c, before):
                u, s = c.parity, L[1]
                rows = kv[u][:].rearrange("p a b -> p (a b)")[:, 0:G * HT].rearrange("p (g d) -> p g d", g=G)
                v.wait_ge(s.e_in[u], c.half * 16 + 16)
                one_hot_t(s, c)
                one_hot(s, c)
                v.wait_ge(s.rows_in[u], c.half * (16 * G) + 16 * G)
                v.tensor_tensor(alpha[u][:, :, 0], rows[:, :, D + 1], tab[u][:, 2 * G:3 * G], ALU.mult).then_inc(s.alpha_ready, 1)
                scan(s, c, 1)
                make_z(s, c, 1)
                make_m(s, c, 1)
                shift(s, c, 1)
                v.wait_ge(s.p_ready, c.number + 1)
                for g in range(G):
                    last = v.tensor_scalar(oh[:, g, :], iota_row[:], tab[u][:, g:g + 1], p_col[:, g:g + 1],
                                           ALU.is_equal, ALU.mult)
                    if g % GROUP == GROUP - 1:
                        last.then_inc(s.weighted_ready, 1)
                for j in range(STEPS):
                    add_parts(s, c, 1, W1, j)

            v.wait_ge(fin_stored[0], windows // 2 * 32)
            v.wait_ge(fin_stored[1], windows // 2 * 32)
            clear_state()
            over_chunks(v, chunks, chain, layer_1)

            def out_tile(c, before):
                u = c.parity
                tot, x1 = sums[u][:, 1, :], msg[u][:, 0, :]
                v.wait_ge(out_loaded[u], c.half * 32 + 32)
                chain.ran(v.tensor_scalar(node_s[u][:, 5:6], tot[:, D:D + 1], 1e-20, None, ALU.max))
                chain.settle()
                chain.ran(v.reciprocal(node_s[u][:, 6:7], node_s[u][:, 5:6]))
                chain.settle()
                v.scalar_tensor_tensor(msg[u][:, 1, :], tot[:, 0:D], node_s[u][:, 6:7], x1, ALU.mult, ALU.add
                                       ).then_inc(out_ready, 1)

            over_chunks(v, windows, chain, out_tile)


_ARGS = ["x", "src_rows", "dst_rows", "t_rows", "tile_last", "msg_t", "node_vec", "time_w", "time_b", "w_all", "b_all",
         "w_edge", "w_score"]


def layout(x, src, dst, edge_attr_64, edge_weight, node_vec, L0_gnn_time_w, L0_gnn_time_b, L0_gnn_Wq, L0_gnn_bq,
           L0_gnn_Wk, L0_gnn_bk, L0_gnn_Wv, L0_gnn_bv, L0_gnn_We, L0_gnn_Wskip, L0_gnn_bskip, L1_gnn_W):
    (n, d), e = x.shape, src.shape[0]
    windows = -(-n // P)
    windows += windows % 2
    tiles = -(-e // TILE)
    chunks = -(-(tiles + windows - 1) // STEPS)
    chunks += chunks % 2
    rows = (-(-chunks * STEPS // P) + 1) * P

    def padded(a, length, value=0):
        full = np.full((length,) + a.shape[1:], value, a.dtype)
        full[:a.shape[0]] = a
        return full

    dst_p = padded(dst, rows * TILE, 1 << 20).reshape(rows, TILE)
    msg = padded(edge_attr_64, rows * TILE).reshape(rows, SUBS, P, -1)
    return {
        "x": padded(x, windows * P),
        "src_rows": padded(src, rows * TILE).reshape(rows, TILE),
        "dst_rows": dst_p,
        "t_rows": padded(edge_weight, rows * TILE).reshape(rows, TILE),
        "tile_last": np.ascontiguousarray(dst_p[:tiles, TILE - 1:].T),
        "msg_t": np.ascontiguousarray(msg.transpose(0, 1, 3, 2)).reshape(rows, -1, P),
        "node_vec": np.ascontiguousarray(padded(node_vec, windows * P).reshape(windows, P).T),
        "time_w": L0_gnn_time_w[None, :], "time_b": L0_gnn_time_b[:, None],
        "w_all": np.concatenate([L0_gnn_Wq, L0_gnn_Wk, L0_gnn_Wv, L0_gnn_Wskip], axis=1),
        "b_all": np.concatenate([L0_gnn_bq, L0_gnn_bk, L0_gnn_bv, L0_gnn_bskip])[None, :],
        "w_edge": L0_gnn_We, "w_score": L1_gnn_W,
    }


def add_program(nc, arrays):
    aps = [nc.dram_tensor(f"in_{k}", arrays[k].shape, mybir.dt.from_np(arrays[k].dtype), kind="ExternalInput").ap()
           for k in _ARGS]
    out = nc.dram_tensor("out_0", arrays["x"].shape, F32, kind="ExternalOutput").ap()
    build(nc, 2, *aps, out)


def kernel(**inputs):
    import concourse.bacc as bacc
    from concourse.bass_utils import run_bass_kernel_spmd

    given = {k: np.asarray(v) for k, v in inputs.items()}
    arrays = layout(**given)
    nc = bacc.Bacc("TRN2", target_bir_lowering=False, num_devices=1)
    add_program(nc, arrays)
    r = run_bass_kernel_spmd(nc, [{f"in_{k}": arrays[k] for k in _ARGS}], core_ids=[0])
    return r.results[0]["out_0"][:given["x"].shape[0]]
```

```python
from contextlib import ExitStack

import numpy as np

import concourse.bass as bass
from concourse import mybir
from concourse.alu_op_type import AluOpType as ALU

F32 = mybir.dt.float32
BF16 = mybir.dt.bfloat16
I32 = mybir.dt.int32
ACT = mybir.ActivationFunctionType
AX = mybir.AxisListType

P = 128
SUBS = 2
TILE = SUBS * P
STEPS = 8
G = STEPS * SUBS
BLOCK_OPS = 10
GROUP = 4
BATCH = 4
BIG = 1.0e30
MAGIC = 12582912.0
TWO_PI_HI = 6.28125
TWO_PI_LO = float(2 * np.pi - 6.28125)
PI_BELOW = 3.1415925
EPS = 1e-5


class Chunk:

    def __init__(self, number, half, parity, slot=None):
        self.number, self.half, self.parity, self.slot = number, half, parity, slot
        self.early = isinstance(number, int) and number < 2

    def back(self, n):
        if isinstance(self.number, int) and self.number < n:
            return None
        return Chunk(self.number - n, self.half + (self.parity - n) // 2, (self.parity - n) % 2,
                     None if self.slot is None else (self.slot - n) % 4)


def chunk_number(c):
    return Chunk(c, c // 2, c % 2, c % 4)


class Chain:

    def __init__(self, engine, semaphore):
        self.engine, self.semaphore, self.base, self.count = engine, semaphore, 0, 0

    def ran(self, instruction):
        instruction.then_inc(self.semaphore, 1)
        self.count += 1

    def settle(self):
        self.engine.wait_ge(self.semaphore, self.base + self.count)

    def loop(self, index, start, per):
        self.base, self.count = index * per + start, 0


def over_chunks(engine, chunks, chain, body, tail=None, turn=2, peel=2):
    assert (chunks - peel) % turn == 0 and turn in (2, 4) and peel % 2 == 0
    for n in range(peel):
        before = chain.count if chain else 0
        body(chunk_number(n), chunk_number(n).back(1))
    if chain:
        per = chain.count - before
        outer, start = chain.base, chain.count
    with engine.Fori(0, (chunks - peel) // turn) as i:
        if chain:
            chain.loop(i, outer + start, turn * per)
        for k in range(peel, peel + turn):
            c = Chunk(i * turn + k, i * (turn // 2) + k // 2, k % 2, k % 4 if turn == 4 else None)
            body(c, c.back(1))
        if chain:
            assert chain.count == turn * per
    if chain:
        chain.base, chain.count = outer + start + (chunks - peel) * per, 0
    if tail:
        tail(chunk_number(chunks - 1))


def registers(nc, engine, row, top):
    return nc.values_load_multi_w_load_instructions(
        row, engines=[engine], min_val=0, max_val=top,
        skip_runtime_bounds_check_because="they are counted on the chip, within the table by construction")[1]


class LayerSemaphores:

    def __init__(self, sem, layer):
        def one(name):
            return sem(f"{name}_{layer}")

        def two(name):
            return [sem(f"{name}_{layer}_{u}") for u in range(2)]

        self.idx_in, self.rows_in = two("idx_in"), two("rows_in")
        self.e_in, self.p_in = two("edge_data_in"), two("tables_in")
        self.sums_stored = two("sums_stored")
        self.angle_turned, self.e_ready = one("angle_turned"), one("e_and_q_ready")
        self.alpha_turned, self.scan_turned = one("alpha_turned"), one("scan_turned")
        self.z_summed, self.m_spread, self.part_ready = one("z_summed"), one("m_spread"), one("part_ready")
        self.angle_ready, self.angle_reduced = one("angle_ready"), one("angle_reduced")
        self.oh_t_ready, self.e_read, self.alpha_ready = one("one_hot_t_ready"), one("e_and_q_read"), one("alpha_ready")
        self.scanned, self.z_ready, self.m_ready = one("scanned"), one("z_ready"), one("m_ready")
        self.decay_ready, self.shift_ready = one("decay_ready"), one("shift_ready")
        self.weighted_ready, self.part_read = one("weighted_ready"), one("part_read")
        self.turns_ready, self.time_ready = one("turns_ready"), one("time_ready")
        self.decay_in, self.p_ready = one("decay_in"), one("p_ready")


def build(nc, heads_0, x, src_rows, dst_rows, t_rows, tile_last, msg_t, node_vec, time_w, time_b, w_all, b_all,
          w_edge, w_score, out):
    n_pad, D = x.shape
    HEADS = heads_0
    CH = D // HEADS
    TDIM = time_w.shape[1]
    MSG = msg_t.shape[1]
    EDGE = TDIM + MSG
    windows, tiles = node_vec.shape[1], tile_last.shape[1]
    node_tiles = n_pad // P
    batches = node_tiles // BATCH
    tile_rows = src_rows.shape[0]
    blocks = tile_rows // P - 1
    chunks = -(-(tiles + windows - 1) // STEPS)
    chunks += (2 - chunks) % 4
    assert batches % 2 == 0 and batches >= 4 and windows <= node_tiles and batches * BATCH == node_tiles and chunks >= 4 and chunks * STEPS <= blocks * P
    NB = blocks * P
    CPB = P // STEPS
    NQ = G // GROUP
    W0 = HEADS * (CH + 1)
    W1 = D + 1
    SCALE = float(CH) ** -0.5
    KV = 2 * D + 1
    HT = D + 2
    TAB = 3 * G + STEPS
    assert TDIM * GROUP == P and EDGE <= P and node_tiles <= P

    def dram(name, shape, dtype):
        return nc.dram_tensor(name, shape, dtype, kind="Internal").ap()

    idx_dram = dram("idx_by_chunk", [blocks * CPB, P, G], I32)
    t_dram = dram("t_by_chunk", [blocks * CPB, P, G], F32)
    tab_dram = dram("tab_by_chunk", [blocks * CPB, P, TAB], F32)
    rel_dram = dram("rel_by_step", [NB, TILE], BF16)
    start_dram = dram("segment_start_by_sub", [NB * SUBS, HEADS, P], F32)
    tile_dram = dram("tile_of_step", [1, NB], I32)
    WINDOW_AT = STEPS - GROUP // SUBS
    window_dram = dram("window_of_step", [1, WINDOW_AT + NB], I32)
    last_dram = dram("last_step_of_window", [P, 1], I32)
    kv_dram = dram("k_v_time_by_node", [n_pad, KV], F32)
    base_dram = dram("x_plus_skip", [n_pad, D], F32)
    h_dram = dram("h_one_score_by_node", [n_pad, HT], F32)
    sums_dram = dram("sums_by_step", [NB, P, W0], F32)
    x1_dram = dram("x_after_layer_0", [n_pad, D], F32)

    with ExitStack() as ctx:
        def sb(name, shape, dtype=F32):
            return ctx.enter_context(nc.sbuf_tensor(name, shape, dtype))

        def sem(name):
            return ctx.enter_context(nc.semaphore(name))

        iota_p = sb("iota_p", [P, 1])
        iota_row = sb("iota_row", [P, P])
        ident = sb("ident", [P, P])
        ones = sb("ones", [P, P])
        w_e = sb("w_e", [EDGE, D])
        time_row = sb("time_row", [P, TDIM])
        time_bias = sb("time_bias", [P, 1])
        time_shift = sb("time_shift", [P, 1])
        magic = sb("magic", [P, 2])
        node_time = sb("node_time", [P, node_tiles])
        b_q = sb("b_q", [P, D])
        stats = [sb(f"stats{u}", [P, BATCH, 6]) for u in range(2)]
        mean_var = [sb(f"mean_var{u}", [P, BATCH, 2]) for u in range(2)]
        std = [sb(f"std{u}", [P, BATCH]) for u in range(2)]
        inv_std = [sb(f"inv_std{u}", [P, BATCH]) for u in range(2)]
        less_mean = [sb(f"less_mean{u}", [P, BATCH]) for u in range(2)]
        weights = [sb(f"weights{u}", [P, BATCH, HEADS]) for u in range(2)]
        score_row = sb("score_row", [P, D])
        q_room = sb("q_room", [P, max(node_tiles * 3 * D // 2, 4 * G * HT)])
        q_rows = q_room[:, 0:node_tiles * 3 * D // 2].bitcast(BF16)
        q_parts = q_rows.rearrange("p (w n d) -> p w n d", n=3, d=D)
        rows_1 = [q_room[:, r * G * HT:(r + 1) * G * HT] for r in range(4)]
        idx = [sb(f"idx{u}", [P, G], I32) for u in range(2)]
        kv = [sb(f"kv{u}", [P, G, KV]) for u in range(2)]
        edge_in = [sb(f"edge_in{u}", [P, G, P]) for u in range(2)]
        t_in = [sb(f"t_in{u}", [P, G]) for u in range(2)]
        rel_b = [sb(f"rel_b{u}", [P, G * P], BF16) for u in range(2)]
        tab = [sb(f"tab{u}", [P, TAB]) for u in range(2)]
        start_b = [sb(f"start_b{u}", [G * HEADS, P]) for u in range(2)]
        oh_t = [sb(f"one_hot_t{u}", [P, G * P], BF16) for u in range(2)]
        ve = [sb(f"ve{u}", [P, G, D]) for u in range(2)]
        alpha = [sb(f"alpha{u}", [P, G, HEADS]) for u in range(2)]
        m_run = [sb(f"m_run{u}", [P, HEADS, STEPS + 1]) for u in range(2)]
        sums = [sb(f"sums{u}", [P, STEPS + 1, W0]) for u in range(2)]
        oh = sb("one_hot", [P, G, P])
        pv = sb("weighted", [P, G, HEADS, CH + 1])
        rel_t = sb("rel_t", [P, G])
        ang = sb("angle", [P, G * TDIM])
        ang_u = sb("angle_u", [P, G * TDIM])
        ang_k = sb("angle_k", [P, G * TDIM])
        prod = sb("prod", [P, GROUP, D])
        ke = sb("ke", [P, GROUP, D])
        seg = sb("seg_max", [P, P])
        z = sb("z", [P, G, HEADS])
        z_parts = sb("z_parts", [P, 3, G, HEADS + 1], BF16)
        zs = sb("z_by_node", [P, G, HEADS + 1])
        absent = sb("absent", [P, G])
        m_step = sb("m_step", [P, HEADS, STEPS])
        m_parts = sb("m_parts", [P, STEPS, 3, HEADS], BF16)
        m_rest = sb("m_rest", [P, STEPS, HEADS])
        decay = [sb(f"decay{u}", [P, STEPS, HEADS]) for u in range(2)]
        shifted = sb("shifted", [P, G, HEADS])
        p_col = sb("p_col", [P, G])

        banks = ctx.enter_context(nc.psum_tensor("banks", [P, 8, 512], F32))
        bank = [banks[:, i, :] for i in range(8)]
        proj_nt = banks[:, 0:BATCH, :]
        e_bank, q_bank, x_bank, part_bank, m_bank = bank[0:2], bank[2:4], bank[4], bank[5:7], bank[7]
        part_bank_1 = bank[0:4]
        MB_BACK, MB_Z, MB_M = P, 2 * P, 2 * P + G * (HEADS + 1)

        vector_chain, scalar_chain = sem("vector_chain"), sem("scalar_chain")
        constants_loaded, iotas_written = sem("constants_loaded"), sem("iotas_written")
        gather_apart, vector_apart, sync_apart = sem("gather_apart"), sem("vector_apart"), sem("sync_apart")
        merge_ready, merge_summed, merge_turned = sem("merge_ready"), sem("merge_summed"), sem("merge_turned")
        sched_ready, sched_stored = sem("sched_ready"), sem("sched_stored")
        idx_col_ready, block_idx_ready = sem("idx_col_ready"), sem("block_idx_ready")
        rows_gathered, rows_decoded, block_turned = sem("rows_gathered"), sem("rows_decoded"), sem("block_turned")
        block_ready, block_stored = sem("block_ready"), sem("block_stored")
        x_loaded = [sem(f"x_loaded{u}") for u in range(2)]
        h_ready, h_turned, h_copied = sem("h_ready"), sem("h_turned"), sem("h_copied")
        x_used, fin_x_used = sem("x_used"), sem("fin_x_used")
        var_ready, std_ready, norm_ready = sem("var_ready"), sem("std_ready"), sem("norm_ready")
        pair_projected, pair_read, node_ready = sem("pair_projected"), sem("pair_read"), sem("node_ready")
        node_stored = [sem(f"node_stored{u}") for u in range(2)]
        fin_loaded = [sem(f"fin_loaded{u}") for u in range(2)]
        fin_var_ready, fin_std_ready, fin_norm_ready = sem("fin_var_ready"), sem("fin_std_ready"), sem("fin_norm_ready")
        fin_h_ready, fin_ready = sem("fin_h_ready"), sem("fin_ready")
        fin_stored = [sem(f"fin_stored{u}") for u in range(2)]
        out_loaded = [sem(f"out_loaded{u}") for u in range(2)]
        out_ready = sem("out_ready")
        out_stored = [sem(f"out_stored{u}") for u in range(2)]
        L = [LayerSemaphores(sem, layer) for layer in range(2)]

        pv_flat = pv[:].rearrange("p g h d -> p (g h d)")
        by_tile = lambda flat, width: flat.rearrange("p (i d) -> p i d", d=width)
        x_nt, h_nt = ([edge_in[u][:, at:at + BATCH, :] for u in range(2)] for at in (0, BATCH))
        turned_nt, base_nt = ([ve[u][:, at:at + BATCH, :] for u in range(2)] for at in (0, BATCH))
        w_in, b_in = (edge_in[0][:, at:at + 4, :].rearrange("p a b -> p (a b)") for at in (2 * BATCH, 2 * BATCH + 4))
        kv_out = [by_tile(pv_flat[:, u * BATCH * KV:(u + 1) * BATCH * KV], KV) for u in range(2)]
        h_out = [by_tile(pv_flat[:, u * BATCH * HT:(u + 1) * BATCH * HT], HT) for u in range(2)]
        tot_nt = [sums[u][:, 0:BATCH, :] for u in range(2)]
        early = kv[0][:].rearrange("p a b -> p (a b)")
        late = kv[1][:].rearrange("p a b -> p (a b)")
        tile_last_b = early[:, 0:tiles].bitcast(I32)
        below = early[:, tiles:2 * tiles]
        passed = early[:, 2 * tiles:2 * tiles + NB]
        iota_s = early[:, 2 * tiles + NB:2 * tiles + 2 * NB]
        ve0 = ve[0][:].rearrange("p a b -> p (a b)")
        ve1 = ve[1][:].rearrange("p a b -> p (a b)")
        win = ve0[:, 0:NB]
        reset = ve0[:, NB:2 * NB]
        sched_i = ve1[:, 0:NB].bitcast(I32)
        sched_w = ve1[:, NB:2 * NB].bitcast(I32)
        merge_c = sb("merge_c", [P, 2])
        last_i = sb("last_i", [P, 1], I32)
        win_col = sb("win_col", [P, blocks])
        tile_col = sb("tile_col", [P, blocks], I32)
        iota_k = sb("iota_k", [P, blocks])
        tile_idx = sb("tile_idx", [P, 1], I32)
        take = lambda at, n: late[:, at:at + n]
        src_r, dst_r = take(0, TILE).bitcast(I32), take(TILE, TILE).bitcast(I32)
        t_r, src_f, rel_f = take(2 * TILE, TILE), take(3 * TILE, TILE), take(4 * TILE, TILE)
        begins, ends = take(5 * TILE, TILE), take(6 * TILE, TILE)
        rel_h = take(7 * TILE, P).bitcast(BF16)
        room = 7 * TILE + P
        idx_b = take(room, CPB * G).bitcast(I32)
        t_b = take(room + CPB * G, CPB * G)
        tab_b = take(room + 2 * CPB * G, CPB * TAB).rearrange("p (c f) -> p c f", c=CPB)

        def alpha_2d(u, heads):
            return alpha[u][:].rearrange("p g h -> p (g h)") if heads == HEADS else alpha[u][:, :, 0]

        oh_of = [oh, ve[0]]

        def upper(one_hots):
            return one_hots[:].bitcast(BF16).rearrange("p g (n two) -> p g n two", two=2)[:, :, :, 1]


        def zs_all(heads):
            return zs[:, :, 0:heads + 1]

        def sums_by_node(c):
            return sums_dram[bass.ds(c.number * STEPS, STEPS)].rearrange("s e f -> e s f")

        block = ctx.enter_context(nc.Block())

        @block.gpsimd
        def _(pool):
            pool.iota(iota_p[:], [[0, 1]], base=0, channel_multiplier=1,
                      allow_small_or_imprecise_dtypes=True).then_inc(iotas_written, 1)
            pool.iota(iota_row[:], [[1, P]], base=0, channel_multiplier=0,
                      allow_small_or_imprecise_dtypes=True).then_inc(iotas_written, 1)
            pool.iota(iota_s, [[1, NB]], base=0, channel_multiplier=0,
                      allow_small_or_imprecise_dtypes=True).then_inc(iotas_written, 1)
            pool.iota(iota_k[:], [[P, blocks]], base=0, channel_multiplier=1,
                      allow_small_or_imprecise_dtypes=True).then_inc(iotas_written, 1)

            with pool.Fori(0, blocks) as k:
                pool.wait_ge(block_idx_ready, k + 1)
                pool.sem_inc(gather_apart, 1)
                for rows, table in ((src_r, src_rows), (dst_r, dst_rows), (t_r, t_rows)):
                    pool.indirect_dma_start(rows, None, table, bass.IndirectOffsetOnAxis(ap=tile_idx[:, 0:1], axis=0)
                                            ).then_inc(rows_gathered, 16)
                pool.wait_ge(rows_gathered, k * 48 + 48)

            def gather(s, c, table, width, rows):
                pool.wait_ge(s.idx_in[c.parity], c.half * 16 + 16)
                pool.sem_inc(gather_apart, 1)
                for g in range(G):
                    pool.indirect_dma_start(rows[:, g * width:(g + 1) * width], None, table,
                                            bass.IndirectOffsetOnAxis(ap=idx[c.parity][:, g:g + 1], axis=0)
                                            ).then_inc(s.rows_in[c.parity], 16)

            def layer_0(c, before):
                if not c.early:
                    pool.wait_ge(L[0].alpha_ready, before.number)
                gather(L[0], c, kv_dram, KV, kv[c.parity][:].rearrange("p a b -> p (a b)"))

            over_chunks(pool, chunks, None, layer_0)

            def layer_1(c, before):
                if not c.early:
                    pool.wait_ge(L[1].alpha_ready, before.number)
                gather(L[1], c, h_dram, HT, rows_1[c.slot])

            over_chunks(pool, chunks, None, layer_1, turn=4)

        @block.sync
        def _(sp):
            for dst, src in ((w_in, w_all), (b_in, b_all.broadcast_to([P, 4 * D])), (time_row[:], time_w.broadcast_to([P, TDIM])), (score_row[:], w_score.broadcast_to([P, D])),
                             (node_time[:, 0:windows], node_vec), (tile_last_b, tile_last.broadcast_to([P, tiles]))):
                sp.dma_start(dst, src).then_inc(constants_loaded, 16)
            sp.dma_start(w_e[:], w_edge).then_inc(constants_loaded, 16)
            for b in range(GROUP):
                sp.dma_start(time_bias[b * TDIM:(b + 1) * TDIM, :], time_b).then_inc(constants_loaded, 16)

            sp.wait_ge(sched_ready, 1)
            sp.dma_start(tile_dram, sched_i[0:1, :]).then_inc(sched_stored, 16)
            sp.dma_start(window_dram[:, WINDOW_AT:WINDOW_AT + NB], sched_w[0:1, :]).then_inc(sched_stored, 16)
            sp.dma_start(last_dram, last_i[:]).then_inc(sched_stored, 16)
            with sp.Fori(0, blocks) as k:
                sp.wait_ge(block_ready, k + 1)
                chunk = bass.ds(k * CPB, CPB)
                sp.dma_start(idx_dram[chunk].rearrange("c e f -> e c f"), idx_b.rearrange("p (c f) -> p c f", c=CPB)
                             ).then_inc(block_stored, 16)
                sp.dma_start(t_dram[chunk].rearrange("c e f -> e c f"), t_b.rearrange("p (c f) -> p c f", c=CPB)
                             ).then_inc(block_stored, 16)
                sp.dma_start(tab_dram[chunk].rearrange("c e f -> e c f"), tab_b).then_inc(block_stored, 16)
                sp.dma_start(rel_dram[bass.ds(k * P, P)], rel_h).then_inc(block_stored, 16)
                for h in range(HEADS):
                    sp.dma_start(start_dram.rearrange("(s b) h e -> s b h e", b=SUBS)[bass.ds(k * P, P), :, h, :],
                                 begins.rearrange("p (b e) -> p b e", b=SUBS)).then_inc(block_stored, 16)

            def nodes(table, c):
                return table[bass.ds(c.number * (BATCH * P), BATCH * P)].rearrange("(i p) f -> p i f", p=P)

            def node_batch(c, before):
                u = c.parity
                if not c.early:
                    sp.wait_ge(h_ready, before.number)
                    sp.wait_ge(x_used, before.number)
                sp.dma_start(x_nt[u], nodes(x, c)).then_inc(x_loaded[u], 16)
                if not c.early:
                    store_nodes(c.back(2))

            def store_nodes(c):
                u = c.parity
                sp.wait_ge(node_ready, c.number + 1)
                sp.dma_start(nodes(kv_dram, c), kv_out[u]).then_inc(node_stored[u], 16)
                sp.dma_start(nodes(base_dram, c), base_nt[u]).then_inc(node_stored[u], 16)

            over_chunks(sp, batches, None, node_batch)
            for c in (batches - 2, batches - 1):
                store_nodes(chunk_number(c))
            for u in range(2):
                sp.wait_ge(node_stored[u], batches // 2 * 32)
            sp.wait_ge(block_stored, blocks * 96)
            sp.wait_ge(sched_stored, 48)

            def load_idx(s, c, before):
                if not c.early:
                    sp.wait_ge(s.rows_in[c.parity], c.half * 16 * G)
                sp.dma_start(idx[c.parity][:], idx_dram[bass.ds(c.number, 1)].rearrange("c e f -> (c e) f")
                             ).then_inc(s.idx_in[c.parity], 16)

            def load_rel(s, c):
                row = rel_dram[bass.ds(c.number * STEPS, STEPS)].rearrange("(o s) e -> o (s e)", o=1)
                sp.dma_start(rel_b[c.parity][:], row.broadcast_to([P, G * P])).then_inc(s.e_in[c.parity], 16)

            def load_tab(s, c, heads):
                rows = start_dram[bass.ds(c.number * G, G), 0:heads, :].rearrange("s h e -> (s h) e") if heads == HEADS \
                    else start_dram[bass.ds(c.number * G, G), 0, :]
                sp.dma_start(tab[c.parity][:], tab_dram[bass.ds(c.number, 1)].rearrange("c e f -> (c e) f")
                             ).then_inc(s.p_in[c.parity], 16)
                sp.dma_start(start_b[c.parity][0:G * heads, :], rows).then_inc(s.p_in[c.parity], 16)

            def layer_0(c, before):
                u, s = c.parity, L[0]
                load_idx(s, c, before)
                if not c.early:
                    sp.wait_ge(s.alpha_ready, before.number)
                sp.dma_start(t_in[u][:], t_dram[bass.ds(c.number, 1)].rearrange("c e f -> (c e) f")
                             ).then_inc(s.e_in[u], 16)
                load_rel(s, c)
                sp.sem_inc(sync_apart, 1)
                tile_of = registers(nc, mybir.EngineType.SP, tile_dram[:, bass.ds(c.number * STEPS, STEPS)], tile_rows - 1)
                for j in range(STEPS):
                    sp.dma_start(edge_in[u][TDIM:EDGE, SUBS * j:SUBS * (j + 1), :],
                                 msg_t[bass.ds(tile_of[j], 1)].rearrange("t m (b e) -> (t m) b e", b=SUBS)
                                 ).then_inc(s.e_in[u], 16)
                if not c.early:
                    sp.wait_ge(s.m_ready, before.number)
                load_tab(s, c, HEADS)

            over_chunks(sp, chunks, None, layer_0)
            for u in range(2):
                sp.wait_ge(L[0].sums_stored[u], chunks // 2 * 16)

            def load_sums(c, rest, what):
                u = c.parity
                sp.dma_start(x_nt[u], nodes(rest, c)).then_inc(what[u], 16)
                sp.sem_inc(sync_apart, 1)
                steps = registers(nc, mybir.EngineType.SP, last_dram[bass.ds(c.number * BATCH, BATCH)].rearrange("a b -> b a"), NB - 1)
                for i in range(BATCH):
                    sp.dma_start(tot_nt[u][:, i, :], sums_dram[bass.ds(steps[i], 1)].rearrange("s e f -> (s e) f")
                                 ).then_inc(what[u], 16)

            def fin_batch(c, before):
                u = c.parity
                if not c.early:
                    sp.wait_ge(fin_x_used, before.number)
                load_sums(c, base_dram, fin_loaded)
                if not c.early:
                    store_fin(c.back(2))

            def store_fin(c):
                u = c.parity
                sp.wait_ge(fin_ready, c.number + 1)
                sp.dma_start(nodes(h_dram, c), h_out[u]).then_inc(fin_stored[u], 16)
                sp.dma_start(nodes(x1_dram, c), base_nt[u]).then_inc(fin_stored[u], 16)

            over_chunks(sp, batches, None, fin_batch)
            for c in (batches - 2, batches - 1):
                store_fin(chunk_number(c))
            for u in range(2):
                sp.wait_ge(fin_stored[u], batches // 2 * 32)

            def layer_1(c, before):
                s = L[1]
                load_idx(s, c, before)
                if not c.early:
                    sp.wait_ge(s.m_ready, before.number)
                load_rel(s, c)
                load_tab(s, c, 1)

            over_chunks(sp, chunks, None, layer_1)
            for u in range(2):
                sp.wait_ge(L[1].sums_stored[u], chunks // 2 * 16)

            def out_batch(c, before):
                u = c.parity
                if not c.early:
                    sp.wait_ge(out_ready, before.number)
                load_sums(c, x1_dram, out_loaded)
                if not c.early:
                    store_out(c.back(2))

            def store_out(c):
                u = c.parity
                sp.wait_ge(out_ready, c.number + 1)
                sp.dma_start(nodes(out, c), h_nt[u]).then_inc(out_stored[u], 16)

            over_chunks(sp, batches, None, out_batch)
            for c in (batches - 2, batches - 1):
                store_out(chunk_number(c))
            for u in range(2):
                sp.wait_ge(out_stored[u], batches // 2 * 16)

        @block.scalar
        def _(act):
            chain = Chain(act, scalar_chain)

            def normalize(c, x, var_sem, std_sem, norm_sem, rows, h_sem):
                u = c.parity
                act.wait_ge(var_sem, c.number + 1)
                act.activation(std[u][:], std[u][:], ACT.Sqrt).then_inc(std_sem, 1)
                act.wait_ge(norm_sem, c.number + 1)
                for i in range(BATCH):
                    last = act.activation(rows[:, i, :], x[:, i, :], ACT.Relu, bias=less_mean[u][:, i:i + 1],
                                          scale=inv_std[u][:, i:i + 1])
                last.then_inc(h_sem, 1)

            def node_batch(c, before):
                u = c.parity
                if not c.early:
                    act.wait_ge(h_turned, before.number)
                normalize(c, x_nt[u], var_ready, std_ready, norm_ready, h_nt[u], h_ready)
                act.wait_ge(h_turned, c.number + 1)
                if not c.early:
                    act.wait_ge(pair_projected, before.number * 2)
                act.activation(turned_nt[u].rearrange("p i n -> p (i n)"), bank[4 + u][:], ACT.Identity).then_inc(h_copied, 1)

            over_chunks(act, batches, None, node_batch)

            def exp_decay(s, c, heads):
                act.wait_ge(s.decay_ready, c.number + 1)
                act.activation(decay[c.parity][:, :, 0:heads], decay[c.parity][:, :, 0:heads], ACT.Exp).then_inc(s.decay_in, 1)


            def time_codes(c):
                s = L[0]
                act.wait_ge(s.angle_turned, c.number + 1)
                if c.back(1):
                    act.wait_ge(s.angle_reduced, c.number)
                chain.ran(act.activation(ang_u[:], x_bank[:], ACT.Identity, bias=time_shift[:, 0:1]))
                chain.settle()
                chain.ran(act.activation(ang_k[:], ang_u[:], ACT.Identity, bias=magic[:, 0:1], scale=float(1 / (2 * np.pi))))
                chain.settle()
                act.activation(ang_k[:], ang_k[:], ACT.Identity, bias=magic[:, 1:2]).then_inc(s.turns_ready, 1)
                act.wait_ge(s.angle_reduced, c.number + 1)
                if c.back(2):
                    act.wait_ge(s.e_ready, c.back(1).number * NQ)
                for b in range(GROUP):
                    last = act.activation(edge_in[c.parity][0:TDIM, b:G:GROUP, :], ang[b * TDIM:(b + 1) * TDIM, :].rearrange(
                        "p (q e) -> p q e", q=NQ), ACT.Sin)
                last.then_inc(s.time_ready, 1)

            def weights_0(c):
                s = L[0]
                exp_decay(s, c, HEADS)
                act.wait_ge(s.shift_ready, c.number + 1)
                act.activation(pv[:, :, :, CH], shifted[:], ACT.Exp).then_inc(s.p_ready, 1)

            def store_sums(s, c):
                act.wait_ge(s.part_read, c.number * STEPS + STEPS)
                act.dma_start(sums_by_node(c), sums[c.parity][:, 1:STEPS + 1, :]).then_inc(s.sums_stored[c.parity], 16)

            def stages_0(ahead, scored):
                if scored:
                    weights_0(scored)
                if ahead:
                    time_codes(ahead)
                if scored:
                    store_sums(L[0], scored)

            def last_0(c):
                stages_0(None, c.back(1))
                stages_0(None, c)

            over_chunks(act, chunks, chain, lambda c, before: stages_0(c, c.back(2)), last_0, peel=4)

            def fin_batch(c, before):
                if not c.early:
                    act.wait_ge(fin_stored[c.parity], c.half * 32)
                normalize(c, base_nt[c.parity], fin_var_ready, fin_std_ready, fin_norm_ready, h_out[c.parity][:, :, 0:D], fin_h_ready)

            over_chunks(act, batches, None, fin_batch)

            def layer_1(c, before):
                s = L[1]
                exp_decay(s, c, 1)
                act.wait_ge(s.shift_ready, c.number + 1)
                act.activation(p_col[:], shifted[:, :, 0], ACT.Exp).then_inc(s.p_ready, 1)
                if before is not None:
                    store_sums(s, before)

            over_chunks(act, chunks, None, layer_1, lambda c: store_sums(L[1], c))

        @block.tensor
        def _(pe):
            pe.wait_ge(merge_ready, 1)
            for half in range(2):
                mm = pe.matmul(part_bank[half][:, 0:NB // 2], ones[0:windows - 1, :],
                               passed[0:windows - 1, half * (NB // 2):(half + 1) * (NB // 2)], start=True, stop=True)
            for k in range(blocks):
                mm = pe.matmul(m_bank[:, k:k + 1], passed[0:windows - 1, k * P:(k + 1) * P], ones[0:windows - 1, 0:1],
                               start=True, stop=True)
            mm.then_inc(merge_summed, 1)

            with pe.Fori(0, blocks) as k:
                pe.wait_ge(rows_decoded, k + 1)
                for n, rows in enumerate((src_f, rel_f, t_r, ends)):
                    for b in range(SUBS):
                        mm = pe.transpose(part_bank[n // 2][:, (n % 2 * SUBS + b) * P:(n % 2 * SUBS + b + 1) * P],
                                          rows[:, b * P:(b + 1) * P], ident[:])
                mm.then_inc(block_turned, 1)

            pe.wait_ge(constants_loaded, 176)

            def node_batch(c, before):
                u = c.parity
                pe.wait_ge(h_ready, c.number + 1)
                if not c.early:
                    pe.wait_ge(h_copied, before.number)
                for i in range(BATCH):
                    mm = pe.transpose(bank[4 + u][:, i * P:(i + 1) * P], h_nt[u][:, i, :], ident[:])
                mm.then_inc(h_turned, 1)
                pe.wait_ge(h_copied, c.number + 1)
                for pair in range(2):
                    if before is not None:
                        pe.wait_ge(pair_read, before.number * 2 + (pair + 1))
                    for i in (2 * pair, 2 * pair + 1):
                        mm = pe.matmul(bank[i][:], turned_nt[u][:, i, :], w_in, start=True, stop=True)
                    mm.then_inc(pair_projected, 1)

            over_chunks(pe, batches, None, node_batch)

            def turn_angles(c):
                s = L[0]
                pe.wait_ge(s.angle_ready, c.number + 1)
                if c.back(1):
                    pe.wait_ge(s.turns_ready, c.number)
                for q in range(NQ):
                    mm = pe.transpose(x_bank[:, q * P:(q + 1) * P], ang[:, q * P:(q + 1) * P], ident[:])
                mm.then_inc(s.angle_turned, 1)

            def edge_group(c, q, win_of):
                u, s = c.parity, L[0]
                eb, qb = e_bank[q % 2], q_bank[q % 2]
                if not (c.early and c.number == 0 and q < 2):
                    pe.wait_ge(s.e_read, c.number * NQ + q - 1)
                for b in range(GROUP):
                    pe.matmul(eb[:, b * D:(b + 1) * D], edge_in[u][0:EDGE, GROUP * q + b, :], w_e[:], start=True, stop=True)
                for b in range(GROUP):
                    g = GROUP * q + b
                    for n in range(3):
                        mm = pe.matmul(qb[:, b * D:(b + 1) * D], oh_t[u][:, g * P:(g + 1) * P],
                                       q_rows[:, bass.ds(win_of[b // SUBS] * (3 * D) + n * D, D)],
                                       start=(n == 0), stop=(n == 2))
                mm.then_inc(s.e_ready, 1)

            def turn_alpha(s, c, heads):
                pe.wait_ge(s.alpha_ready, c.number + 1)
                pe.transpose(m_bank[0:G * heads, 0:P], alpha_2d(c.parity, heads), ident[:]).then_inc(s.alpha_turned, 1)

            def turn_scan(s, c, heads):
                pe.wait_ge(s.scanned, c.number + 1)
                pe.transpose(m_bank[:, MB_BACK:MB_BACK + P], seg[:], ident[:]).then_inc(s.scan_turned, 1)

            def sum_z(s, c, heads, one_hots):
                pe.wait_ge(s.z_ready, c.number + 1)
                n = heads + 1
                for g in range(G):
                    for part in range(3):
                        mm = pe.matmul(m_bank[:, MB_Z + g * n:MB_Z + (g + 1) * n], upper(one_hots)[:, g, :], z_parts[:, part, g, 0:n],
                                       start=(part == 0), stop=(part == 2))
                mm.then_inc(s.z_summed, 1)

            def spread_m(s, c, heads):
                pe.wait_ge(s.m_ready, c.number + 1)
                for g in range(G):
                    for part in range(3):
                        mm = pe.matmul(m_bank[:, MB_M + g * heads:MB_M + (g + 1) * heads], oh_t[c.parity][:, g * P:(g + 1) * P],
                                       m_parts[:, g // SUBS, part, 0:heads], start=(part == 0), stop=(part == 2))
                mm.then_inc(s.m_spread, 1)

            def sum_parts(s, c, steps, width, one_hots, rows, into):
                for j in steps:
                    if j % 2 == 0:
                        pe.wait_ge(s.weighted_ready, c.number * NQ + (j // 2 + 1))
                    if not (isinstance(c.number, int) and c.number == 0 and j < len(into)):
                        pe.wait_ge(s.part_read, c.number * STEPS + (j + 1 - len(into)))
                    for b in range(SUBS):
                        g = SUBS * j + b
                        mm = pe.matmul(into[j % len(into)][:, 0:width], one_hots[:, g, :], rows(g),
                                       start=(b == 0), stop=(b == SUBS - 1))
                    mm.then_inc(s.part_ready, 1)

            def weighted_rows(g):
                return pv[:, g, :, :].rearrange("p h d -> p (h d)")

            def sums_0(c, steps):
                sum_parts(L[0], c, steps, W0, oh, weighted_rows, part_bank)

            def stages_0(ahead, c, scored):
                s = L[0]
                per = GROUP // SUBS
                late = STEPS - per if c else 0
                if c or ahead:
                    first = c.number * STEPS + per if c else ahead.number * STEPS
                    steps = bass.ds(first + WINDOW_AT, late + (per if ahead else 0))
                    win_of = registers(nc, mybir.EngineType.PE, window_dram[:, steps], windows - 1)
                if scored:
                    turn_scan(s, scored, HEADS)
                if c:
                    edge_group(c, 1, win_of)
                if scored:
                    sum_z(s, scored, HEADS, oh)
                if c:
                    edge_group(c, 2, win_of[per:])
                if scored:
                    spread_m(s, scored, HEADS)
                if c:
                    edge_group(c, 3, win_of[2 * per:])
                if ahead:
                    turn_angles(ahead)
                if scored:
                    sums_0(scored, (0, 1))
                if c:
                    turn_alpha(s, c, HEADS)
                if scored:
                    sums_0(scored, range(2, STEPS))
                if ahead:
                    pe.wait_ge(s.time_ready, ahead.number + 1)
                    pe.wait_ge(s.oh_t_ready, ahead.number + 1)
                    pe.wait_ge(s.e_in[ahead.parity], ahead.half * (16 * (STEPS + 2)) + 16 * (STEPS + 2))
                    edge_group(ahead, 0, win_of[late:])

            def last_0(c):
                stages_0(None, c, c.back(1))
                stages_0(None, None, c)

            pe.wait_ge(sched_stored, 48)
            over_chunks(pe, chunks, None, lambda c, before: stages_0(c, before, c.back(2)), last_0, peel=4)

            def sums_1(c, steps):
                sum_parts(L[1], c, steps, W1, oh_of[c.parity], lambda g: rows_1[c.slot][:, g * HT:g * HT + W1], part_bank_1)

            def layer_1(c, before):
                s = L[1]
                turn_alpha(s, c, 1)
                if before is not None:
                    sums_1(before, (0, 1))
                turn_scan(s, c, 1)
                if before is not None:
                    sums_1(before, (2, 3))
                sum_z(s, c, 1, oh_of[c.parity])
                if before is not None:
                    sums_1(before, (4, 5))
                spread_m(s, c, 1)
                if before is not None:
                    sums_1(before, (6, 7))

            over_chunks(pe, chunks, None, layer_1, lambda c: sums_1(c, range(STEPS)), turn=4)

        @block.vector
        def _(v):
            chain = Chain(v, vector_chain)

            def statistics(xt, u, var_sem):
                for i in range(BATCH):
                    chain.ran(v.bn_stats(stats[u][:, i, :], xt[:, i, :]))
                chain.settle()
                v.sem_inc(vector_apart, 1)
                for i in range(BATCH):
                    chain.ran(v.bn_aggr(mean_var[u][:, i, :], stats[u][:, i, :]))
                chain.settle()
                v.tensor_scalar(std[u][:], mean_var[u][:, :, 1], EPS, None, ALU.add).then_inc(var_sem, 1)

            def invert(c, std_sem, norm_sem):
                u = c.parity
                v.wait_ge(std_sem, c.number + 1)
                chain.ran(v.reciprocal(inv_std[u][:], std[u][:]))
                chain.settle()
                v.scalar_tensor_tensor(less_mean[u][:], mean_var[u][:, :, 0], -1.0, inv_std[u][:], ALU.mult, ALU.mult
                                       ).then_inc(norm_sem, 1)

            v.wait_ge(iotas_written, 4)
            chain.ran(v.tensor_scalar(ident[:], iota_row[:], iota_p[:, 0:1], None, ALU.is_equal))
            chain.ran(v.memset(ones[:], 1.0))
            chain.ran(v.memset(magic[:, 0:1], MAGIC))
            chain.ran(v.memset(magic[:, 1:2], -MAGIC))
            chain.ran(v.memset(seg[:], 0.0))
            v.wait_ge(constants_loaded, 176)
            chain.ran(v.tensor_scalar(b_q[:], b_in[:, 0:D], SCALE, None, ALU.mult))
            if node_tiles > windows:
                chain.ran(v.memset(node_time[:, windows:node_tiles], 0.0))
            chain.ran(v.tensor_scalar(time_shift[:], time_bias[:], float(np.pi / 2), None, ALU.add))
            chain.ran(v.tensor_scalar(merge_c[:, 0:1], iota_p[:], float(P), float(P), ALU.mult, ALU.add))
            chain.settle()
            chain.ran(v.tensor_scalar(below, tile_last_b, merge_c[:, 0:1], None, ALU.is_lt))
            chain.settle()
            chain.ran(v.tensor_reduce(merge_c[:, 1:2], below, AX.X, ALU.add))
            chain.settle()
            chain.ran(v.tensor_tensor(merge_c[:, 0:1], merge_c[:, 1:2], iota_p[:], ALU.add))
            chain.settle()
            chain.ran(v.tensor_scalar(merge_c[:, 1:2], iota_p[:], float(windows - 1), float(chunks * STEPS),
                                      ALU.is_ge, ALU.mult))
            chain.settle()
            chain.ran(v.tensor_scalar(merge_c[:, 1:2], merge_c[:, 1:2], merge_c[:, 0:1], float(chunks * STEPS - 1),
                                      ALU.add, ALU.min))
            chain.settle()
            chain.ran(v.tensor_copy(last_i[:], merge_c[:, 1:2]))
            v.tensor_scalar(passed, iota_s, merge_c[:, 0:1], None, ALU.is_gt).then_inc(merge_ready, 1)
            v.wait_ge(merge_summed, 1)
            for half in range(2):
                cut = slice(half * (NB // 2), (half + 1) * (NB // 2))
                chain.ran(v.tensor_copy(win[:, cut], part_bank[half][:, 0:NB // 2]))
            chain.ran(v.tensor_scalar(win_col[:], m_bank[:, 0:blocks], float(P), None, ALU.mult))
            chain.ran(v.tensor_tensor(tile_col[:], iota_k[:], m_bank[:, 0:blocks], ALU.subtract))
            chain.settle()
            chain.ran(v.tensor_copy(sched_w[0:1, :], win[0:1, :]))
            chain.ran(v.tensor_tensor(reset[:, 1:NB], win[:, 1:NB], win[:, 0:NB - 1], ALU.not_equal))
            chain.ran(v.memset(reset[:, 0:1], 0.0))
            chain.settle()
            chain.ran(v.tensor_scalar(reset, reset, -2.0 * BIG, None, ALU.mult))
            v.tensor_tensor(sched_i[0:1, :], iota_s[0:1, :], win[0:1, :], ALU.subtract).then_inc(sched_ready, 1)
            begins_3, ends_3 = (r.rearrange("p (b e) -> p b e", b=SUBS) for r in (begins, ends))
            rel_3 = rel_f.rearrange("p (b e) -> p b e", b=SUBS)
            chain.ran(v.memset(begins_3[:, :, 0:1], -BIG))
            chain.ran(v.memset(ends_3[:, :, P - 1:P], 1.0))
            chain.settle()

            outer, first = chain.base, chain.count
            with v.Fori(0, blocks) as k:
                chain.loop(k, outer + first, BLOCK_OPS)
                v.tensor_copy(tile_idx[:], tile_col[:, bass.ds(k, 1)]).then_inc(block_idx_ready, 1)
                v.wait_ge(rows_gathered, k * 48 + 48)
                chain.ran(v.tensor_copy(src_f, src_r))
                chain.ran(v.tensor_scalar(rel_f, dst_r, win_col[:, bass.ds(k, 1)], None, ALU.subtract))
                chain.settle()
                chain.ran(v.tensor_scalar(rel_h, rel_f, -1.0, float(P), ALU.max, ALU.min))
                chain.ran(v.tensor_tensor(ends_3[:, :, 0:P - 1], rel_3[:, :, 0:P - 1], rel_3[:, :, 1:P], ALU.not_equal))
                chain.settle()
                v.tensor_scalar(begins_3[:, :, 1:P], ends_3[:, :, 0:P - 1], -BIG, None, ALU.mult).then_inc(rows_decoded, 1)
                v.wait_ge(block_turned, k + 1)

                def turned(n):
                    return part_bank[n // 2][:, n % 2 * TILE:(n % 2 + 1) * TILE].rearrange("p (b c s) -> p c s b", b=SUBS, s=STEPS)

                def column(view, at):
                    return view[:, :, at:at + G].rearrange("p c (s b) -> p c s b", b=SUBS)

                idx_3 = idx_b.rearrange("p (c f) -> p c f", c=CPB)
                t_3 = t_b.rearrange("p (c f) -> p c f", c=CPB)
                chain.ran(v.tensor_copy(column(idx_3, 0), turned(0)))
                chain.ran(v.tensor_copy(column(tab_b, 0), turned(1)))
                chain.ran(v.tensor_copy(column(t_3, 0), turned(2)))
                chain.ran(v.tensor_copy(column(tab_b, G), turned(3)))
                chain.ran(v.tensor_copy(tab_b[:, :, 3 * G:TAB],
                                        reset[:, bass.ds(k * P, P)].rearrange("p (c s) -> p c s", s=STEPS)))
                chain.settle()
                chain.ran(v.tensor_scalar(tab_b[:, :, 2 * G:3 * G], tab_b[:, :, 0:G], 0.0, None, ALU.is_ge))
                chain.settle()
                v.scalar_tensor_tensor(tab_b[:, :, 2 * G:3 * G], tab_b[:, :, 0:G], float(P), tab_b[:, :, 2 * G:3 * G],
                                       ALU.is_lt, ALU.mult).then_inc(block_ready, 1)
                v.wait_ge(block_stored, k * 96 + 96)
                assert chain.count == BLOCK_OPS
            chain.base, chain.count = outer + first + blocks * BLOCK_OPS, 0

            def project_pair(c, pair):
                u, tiles_2 = c.parity, slice(2 * pair, 2 * pair + 2)
                v.wait_ge(pair_projected, c.number * 2 + (pair + 1))
                q, rest = prod[:, 0:2, :], prod[:, 2:4, :]
                both = lambda row: row.unsqueeze(1).broadcast_to([P, 2, row.shape[-1]])
                product = lambda at, n: proj_nt[:, 2 * pair:2 * pair + 2, at:at + n]
                hi, mid, lo = (q_parts[:, bass.ds(c.number * BATCH + 2 * pair, 2), n, :] for n in range(3))
                chain.ran(v.scalar_tensor_tensor(q, product(0, D), SCALE, both(b_q[:]), ALU.mult, ALU.add))
                chain.ran(v.tensor_tensor(kv_out[u][:, tiles_2, 0:2 * D], product(D, 2 * D), both(b_in[:, D:3 * D]), ALU.add))
                chain.settle()
                chain.ran(v.tensor_copy(hi, q))
                v.wait_ge(x_used, c.number + 1)
                v.tensor_tensor(base_nt[u][:, tiles_2, :], base_nt[u][:, tiles_2, :], product(3 * D, D), ALU.add
                                ).then_inc(pair_read, 1)
                chain.settle()
                chain.ran(v.tensor_tensor(rest, q, hi, ALU.subtract))
                chain.ran(v.tensor_copy(kv_out[u][:, tiles_2, 2 * D], node_time[:, bass.ds(c.number * BATCH + 2 * pair, 2)]))
                chain.settle()
                chain.ran(v.tensor_copy(mid, rest))
                chain.settle()
                if pair == 0:
                    chain.ran(v.tensor_tensor(lo, rest, mid, ALU.subtract))
                else:
                    v.wait_ge(pair_read, c.number * 2 + 2)
                    v.tensor_tensor(lo, rest, mid, ALU.subtract).then_inc(node_ready, 1)

            def node_batch(c, before):
                u = c.parity
                v.wait_ge(x_loaded[u], c.half * 16 + 16)
                statistics(x_nt[u], u, var_ready)
                if before is not None:
                    project_pair(before, 0)
                invert(c, std_ready, norm_ready)
                if not c.early:
                    v.wait_ge(node_stored[u], c.half * 32)
                v.tensor_tensor(base_nt[u], x_nt[u], b_in[:, 3 * D:4 * D].unsqueeze(1).broadcast_to([P, BATCH, D]), ALU.add
                                ).then_inc(x_used, 1)
                if before is not None:
                    project_pair(before, 1)

            def last_nodes(c):
                project_pair(c, 0)
                project_pair(c, 1)

            v.wait_ge(sched_stored, 48)
            over_chunks(v, batches, chain, node_batch, last_nodes)

            def clear_state(heads):
                chain.ran(v.memset(z_parts[:, 1:3, :, heads:heads + 1], 0.0))
                chain.ran(v.memset(m_run[1][:, :, STEPS:STEPS + 1], -BIG))
                chain.ran(v.memset(sums[1][:, STEPS, :], 0.0))
                chain.settle()

            def one_hot_t(s, c):
                v.tensor_scalar(oh_t[c.parity][:], rel_b[c.parity][:], iota_p[:, 0:1], None, ALU.is_equal
                                ).then_inc(s.oh_t_ready, 1)

            def one_hot(s, c, one_hots):
                v.wait_ge(s.p_in[c.parity], c.half * 32 + 32)
                chain.ran(v.tensor_tensor(one_hots[:], iota_row[:].unsqueeze(1).broadcast_to([P, G, P]),
                                          tab[c.parity][:, 0:G].unsqueeze(2).broadcast_to([P, G, P]), ALU.is_equal))

            def scan(s, c, heads):
                n = G * heads
                v.wait_ge(s.p_in[c.parity], c.half * 32 + 32)
                v.wait_ge(s.alpha_turned, c.number + 1)
                v.tensor_tensor_scan(seg[0:n, :], start_b[c.parity][0:n, :], m_bank[0:n, 0:P], -BIG, ALU.add, ALU.max
                                     ).then_inc(s.scanned, 1)

            def make_z(s, c, heads):
                ends_c = tab[c.parity][:, G:2 * G].unsqueeze(2)
                v.wait_ge(s.scan_turned, c.number + 1)
                back = m_bank[:, MB_BACK:MB_BACK + G * heads].rearrange("p (g h) -> p g h", h=heads)
                hi, mid, lo = (z_parts[:, n, :, 0:heads] for n in range(3))
                zf = z[:, :, 0:heads]
                chain.ran(v.tensor_tensor(zf, back, ends_c.broadcast_to([P, G, heads]), ALU.mult))
                chain.ran(v.tensor_copy(z_parts[:, 0, :, heads:heads + 1], ends_c))
                chain.settle()
                chain.ran(v.tensor_copy(hi, zf))
                chain.settle()
                chain.ran(v.tensor_tensor(zf, zf, hi, ALU.subtract))
                chain.settle()
                chain.ran(v.tensor_copy(mid, zf))
                chain.settle()
                v.tensor_tensor(lo, zf, mid, ALU.subtract).then_inc(s.z_ready, 1)

            def make_m(s, c, heads):
                m, old = m_run[c.parity], m_run[1 - c.parity]
                zn, t = zs_all(heads), tab[c.parity]
                v.wait_ge(s.z_summed, c.number + 1)
                chain.ran(v.tensor_copy(zn, m_bank[:, MB_Z:MB_Z + G * (heads + 1)].rearrange("p (g n) -> p g n", g=G)))
                chain.ran(v.tensor_copy(m[:, 0:heads, 0:1], old[:, 0:heads, STEPS:STEPS + 1]))
                chain.settle()
                chain.ran(v.tensor_scalar(absent[:], zn[:, :, heads], -1.0, BIG, ALU.add, ALU.mult))
                chain.settle()
                chain.ran(v.tensor_tensor(zn[:, :, 0:heads], zn[:, :, 0:heads],
                                          absent[:].unsqueeze(2).broadcast_to([P, G, heads]), ALU.add))
                chain.settle()
                pair = zn.rearrange("p (s b) n -> p b n s", b=SUBS)
                chain.ran(v.tensor_tensor(m_step[:, 0:heads, :], pair[:, 0, 0:heads, :], pair[:, 1, 0:heads, :], ALU.max))
                chain.settle()
                for h in range(heads):
                    chain.ran(v.tensor_tensor_scan(m[:, h, 1:STEPS + 1], t[:, 3 * G:TAB], m_step[:, h, :],
                                                   m[:, h, 0:1], ALU.add, ALU.max))
                chain.settle()
                now = m[:, 0:heads, 1:STEPS + 1].rearrange("p h s -> p s h")
                past = m[:, 0:heads, 0:STEPS].rearrange("p h s -> p s h")
                hi, mid, lo = (m_parts[:, :, n, 0:heads] for n in range(3))
                rest, dec = m_rest[:, :, 0:heads], decay[c.parity][:, :, 0:heads]
                chain.ran(v.tensor_copy(hi, now))
                chain.ran(v.tensor_tensor(dec, past, t[:, 3 * G:TAB].unsqueeze(2).broadcast_to([P, STEPS, heads]), ALU.add))
                chain.settle()
                chain.ran(v.tensor_tensor(rest, now, hi, ALU.subtract))
                v.tensor_tensor(dec, dec, now, ALU.subtract).then_inc(s.decay_ready, 1)
                chain.settle()
                chain.ran(v.tensor_copy(mid, rest))
                chain.settle()
                v.tensor_tensor(lo, rest, mid, ALU.subtract).then_inc(s.m_ready, 1)

            def shift(s, c, heads):
                v.wait_ge(s.m_spread, c.number + 1)
                spread = m_bank[:, MB_M:MB_M + G * heads].rearrange("p (g h) -> p g h", h=heads)
                v.tensor_tensor(shifted[:, :, 0:heads], alpha[c.parity][:, :, 0:heads], spread, ALU.subtract
                                ).then_inc(s.shift_ready, 1)

            def add_parts(s, c, heads, width, j, banks_used):
                S = sums[c.parity]
                past = S[:, j, :] if j else sums[1 - c.parity][:, STEPS, :]
                if j == 0:
                    v.wait_ge(s.decay_in, c.number + 1)
                    if not c.early:
                        v.wait_ge(s.sums_stored[c.parity], c.half * 16)
                if not (isinstance(c.number, int) and c.number == 0 and j == 0):
                    v.wait_ge(s.part_read, c.number * STEPS + j)
                v.wait_ge(s.part_ready, c.number * STEPS + (j + 1))
                n = width // heads
                for h in range(heads):
                    last = v.scalar_tensor_tensor(S[:, j + 1, h * n:(h + 1) * n], past[:, h * n:(h + 1) * n],
                                                  decay[c.parity][:, j, h:h + 1], banks_used[j % len(banks_used)][:, h * n:(h + 1) * n],
                                                  ALU.mult, ALU.add)
                last.then_inc(s.part_read, 1)

            def angles(c):
                u, s = c.parity, L[0]
                v.wait_ge(s.rows_in[u], c.half * (16 * G) + 16 * G)
                v.wait_ge(s.e_in[u], c.half * (16 * (STEPS + 2)) + 16 * (STEPS + 2))
                chain.ran(v.tensor_tensor(rel_t[:], kv[u][:, :, 2 * D], t_in[u][:], ALU.subtract))
                chain.settle()
                if c.back(1):
                    v.wait_ge(s.time_ready, c.number)
                v.tensor_tensor(ang[:].rearrange("p (g d) -> p g d", g=G),
                                time_row[:].unsqueeze(1).broadcast_to([P, G, TDIM]),
                                rel_t[:].unsqueeze(2).broadcast_to([P, G, TDIM]), ALU.mult).then_inc(s.angle_ready, 1)

            def reduce_angles(c):
                s = L[0]
                v.wait_ge(s.turns_ready, c.number + 1)
                chain.ran(v.scalar_tensor_tensor(ang[:], ang_k[:], -TWO_PI_HI, ang_u[:], ALU.mult, ALU.add))
                chain.settle()
                chain.ran(v.scalar_tensor_tensor(ang[:], ang_k[:], -TWO_PI_LO, ang[:], ALU.mult, ALU.add))
                chain.settle()
                v.tensor_scalar(ang[:], ang[:], PI_BELOW, -PI_BELOW, ALU.min, ALU.max).then_inc(s.angle_reduced, 1)

            def score_group(c, q):
                u, s = c.parity, L[0]
                subs = slice(GROUP * q, GROUP * (q + 1))
                e = e_bank[q % 2][:].rearrange("p (g d) -> p g d", g=GROUP)
                qd = q_bank[q % 2][:].rearrange("p (g d) -> p g d", g=GROUP)
                v.wait_ge(s.e_ready, c.number * NQ + (q + 1))
                chain.ran(v.tensor_tensor(ke[:], kv[u][:, subs, 0:D], e, ALU.add))
                chain.ran(v.tensor_tensor(ve[u][:, subs, :], kv[u][:, subs, D:2 * D], e, ALU.add))
                chain.settle()
                v.tensor_tensor(prod[:], ke[:], qd, ALU.mult).then_inc(s.e_read, 1)
                v.wait_ge(s.e_read, c.number * NQ + (q + 1))
                last = v.tensor_reduce(alpha[u][:, subs, :], prod[:].rearrange("p g (h d) -> p g h d", h=HEADS), AX.X, ALU.add)
                if q == NQ - 1:
                    chain.settle()
                    last.then_inc(s.alpha_ready, 1)
                else:
                    chain.ran(last)

            def weigh_group(c, q):
                s = L[0]
                subs = slice(GROUP * q, GROUP * (q + 1))
                v.tensor_tensor(pv[:, subs, :, 0:CH], ve[c.parity][:, subs, :].rearrange("p g (h d) -> p g h d", h=HEADS),
                                pv[:, subs, :, CH:CH + 1].broadcast_to([P, GROUP, HEADS, CH]), ALU.mult
                                ).then_inc(s.weighted_ready, 1)

            def sums_0(c, steps):
                for j in steps:
                    add_parts(L[0], c, HEADS, W0, j, part_bank)

            def stages_0(ahead, c, scored):
                s = L[0]
                if scored:
                    scan(s, scored, HEADS)
                    one_hot(s, scored, oh)
                    make_z(s, scored, HEADS)
                if c:
                    score_group(c, 0)
                    score_group(c, 1)
                if scored:
                    make_m(s, scored, HEADS)
                if c:
                    score_group(c, 2)
                if scored:
                    shift(s, scored, HEADS)
                if ahead:
                    angles(ahead)
                if scored:
                    v.wait_ge(s.p_ready, scored.number + 1)
                    weigh_group(scored, 0)
                    weigh_group(scored, 1)
                if c:
                    score_group(c, 3)
                if scored:
                    sums_0(scored, (0, 1))
                if ahead:
                    reduce_angles(ahead)
                if scored:
                    weigh_group(scored, 2)
                    sums_0(scored, (2, 3))
                if ahead:
                    one_hot_t(s, ahead)
                if scored:
                    weigh_group(scored, 3)
                    sums_0(scored, range(4, STEPS))

            def last_0(c):
                stages_0(None, c, c.back(1))
                stages_0(None, None, c)

            clear_state(HEADS)
            over_chunks(v, chunks, chain, lambda c, before: stages_0(c, before, c.back(2)), last_0, peel=4)

            def fin_batch(c, before):
                u = c.parity
                tot = tot_nt[u].rearrange("p i (h d) -> p i h d", h=HEADS)
                x1 = base_nt[u].rearrange("p i (h d) -> p i h d", h=HEADS)
                v.wait_ge(fin_loaded[u], c.half * (16 * (BATCH + 1)) + 16 * (BATCH + 1))
                chain.ran(v.tensor_scalar(weights[u][:], tot[:, :, :, CH], 1e-16, None, ALU.add))
                chain.settle()
                chain.ran(v.reciprocal(weights[u][:], weights[u][:]))
                chain.settle()
                if not c.early:
                    v.wait_ge(fin_stored[u], c.half * 32)
                chain.ran(v.tensor_tensor(x1, tot[:, :, :, 0:CH], weights[u][:].unsqueeze(3).broadcast_to([P, BATCH, HEADS, CH]), ALU.mult))
                chain.settle()
                v.tensor_tensor(base_nt[u], base_nt[u], x_nt[u], ALU.add).then_inc(fin_x_used, 1)
                v.wait_ge(fin_x_used, c.number + 1)
                statistics(base_nt[u], u, fin_var_ready)
                if before is not None:
                    score_nodes(before)
                invert(c, fin_std_ready, fin_norm_ready)

            def score_nodes(c):
                u = c.parity
                rows = h_out[u]
                v.wait_ge(fin_h_ready, c.number + 1)
                chain.ran(v.memset(rows[:, :, D:D + 1], 1.0))
                for i in range(BATCH):
                    if i == BATCH - 1:
                        chain.settle()
                    last = v.tensor_tensor_reduce(prod[:, i, :], rows[:, i, 0:D], score_row[:], 1.0, 0.0, ALU.mult, ALU.add,
                                                  rows[:, i, D + 1:HT])
                    if i < BATCH - 1:
                        chain.ran(last)
                last.then_inc(fin_ready, 1)
                v.wait_ge(fin_ready, c.number + 1)

            over_chunks(v, batches, chain, fin_batch, score_nodes)

            def weigh_1(c):
                one_hots = oh_of[c.parity]
                v.wait_ge(L[1].p_ready, c.number + 1)
                for q in range(NQ):
                    subs = slice(GROUP * q, GROUP * (q + 1))
                    v.tensor_tensor(one_hots[:, subs, :], one_hots[:, subs, :],
                                    p_col[:, subs].unsqueeze(2).broadcast_to([P, GROUP, P]), ALU.mult
                                    ).then_inc(L[1].weighted_ready, 1)

            def add_parts_1(c, steps):
                for j in steps:
                    add_parts(L[1], c, 1, W1, j, part_bank_1)

            def layer_1(c, before):
                u, s = c.parity, L[1]
                rows = rows_1[c.slot].rearrange("p (g d) -> p g d", g=G)
                v.wait_ge(s.e_in[u], c.half * 16 + 16)
                one_hot_t(s, c)
                one_hot(s, c, oh_of[u])
                v.wait_ge(s.rows_in[u], c.half * (16 * G) + 16 * G)
                v.tensor_tensor(alpha[u][:, :, 0], rows[:, :, D + 1], tab[u][:, 2 * G:3 * G], ALU.mult).then_inc(s.alpha_ready, 1)
                if before is not None:
                    weigh_1(before)
                scan(s, c, 1)
                if before is not None:
                    add_parts_1(before, (0, 1))
                make_z(s, c, 1)
                if before is not None:
                    add_parts_1(before, (2, 3))
                make_m(s, c, 1)
                if before is not None:
                    add_parts_1(before, (4, 5))
                shift(s, c, 1)
                if before is not None:
                    add_parts_1(before, (6, 7))

            def last_1(c):
                weigh_1(c)
                add_parts_1(c, range(STEPS))

            for u in range(2):
                v.wait_ge(fin_stored[u], batches // 2 * 32)
            clear_state(1)
            over_chunks(v, chunks, chain, layer_1, last_1, turn=4)

            def out_batch(c, before):
                u = c.parity
                v.wait_ge(out_loaded[u], c.half * (16 * (BATCH + 1)) + 16 * (BATCH + 1))
                w = weights[u][:, :, 0]
                chain.ran(v.tensor_scalar(w, tot_nt[u][:, :, D], 1e-20, None, ALU.max))
                chain.settle()
                chain.ran(v.reciprocal(w, w))
                chain.settle()
                if not c.early:
                    v.wait_ge(out_stored[u], c.half * 16)
                chain.ran(v.tensor_tensor(h_nt[u], tot_nt[u][:, :, 0:D], w.unsqueeze(2).broadcast_to([P, BATCH, D]), ALU.mult))
                chain.settle()
                v.tensor_tensor(h_nt[u], h_nt[u], x_nt[u], ALU.add).then_inc(out_ready, 1)

            over_chunks(v, batches, chain, out_batch)


_ARGS = ["x", "src_rows", "dst_rows", "t_rows", "tile_last", "msg_t", "node_vec", "time_w", "time_b", "w_all", "b_all",
         "w_edge", "w_score"]


def layout(x, src, dst, edge_attr_64, edge_weight, node_vec, L0_gnn_time_w, L0_gnn_time_b, L0_gnn_Wq, L0_gnn_bq,
           L0_gnn_Wk, L0_gnn_bk, L0_gnn_Wv, L0_gnn_bv, L0_gnn_We, L0_gnn_Wskip, L0_gnn_bskip, L1_gnn_W):
    (n, d), e = x.shape, src.shape[0]
    windows = -(-n // P)
    node_tiles = -(-windows // (2 * BATCH)) * (2 * BATCH)
    tiles = -(-e // TILE)
    chunks = -(-(tiles + windows - 1) // STEPS)
    chunks += (2 - chunks) % 4
    rows = (-(-chunks * STEPS // P) + 1) * P

    def padded(a, length, value=0):
        full = np.full((length,) + a.shape[1:], value, a.dtype)
        full[:a.shape[0]] = a
        return full

    dst_p = padded(dst, rows * TILE, 1 << 20).reshape(rows, TILE)
    msg = padded(edge_attr_64, rows * TILE).reshape(rows, TILE, -1)
    return {
        "x": padded(x, node_tiles * P),
        "src_rows": padded(src, rows * TILE).reshape(rows, TILE),
        "dst_rows": dst_p,
        "t_rows": padded(edge_weight, rows * TILE).reshape(rows, TILE),
        "tile_last": np.ascontiguousarray(dst_p[:tiles, TILE - 1:].T),
        "msg_t": np.ascontiguousarray(msg.transpose(0, 2, 1)),
        "node_vec": np.ascontiguousarray(padded(node_vec, windows * P).reshape(windows, P).T),
        "time_w": L0_gnn_time_w[None, :], "time_b": L0_gnn_time_b[:, None],
        "w_all": np.concatenate([L0_gnn_Wq, L0_gnn_Wk, L0_gnn_Wv, L0_gnn_Wskip], axis=1),
        "b_all": np.concatenate([L0_gnn_bq, L0_gnn_bk, L0_gnn_bv, L0_gnn_bskip])[None, :],
        "w_edge": L0_gnn_We, "w_score": L1_gnn_W,
    }


def add_program(nc, arrays):
    aps = [nc.dram_tensor(f"in_{k}", arrays[k].shape, mybir.dt.from_np(arrays[k].dtype), kind="ExternalInput").ap()
           for k in _ARGS]
    out = nc.dram_tensor("out_0", arrays["x"].shape, F32, kind="ExternalOutput").ap()
    build(nc, 2, *aps, out)


def kernel(**inputs):
    import concourse.bacc as bacc
    from concourse.bass_utils import run_bass_kernel_spmd

    given = {k: np.asarray(v) for k, v in inputs.items()}
    arrays = layout(**given)
    nc = bacc.Bacc("TRN2", target_bir_lowering=False, num_devices=1)
    add_program(nc, arrays)
    r = run_bass_kernel_spmd(nc, [{f"in_{k}": arrays[k] for k in _ARGS}], core_ids=[0])
    return r.results[0]["out_0"][:given["x"].shape[0]]
```
